# Optimizing a Trainium2 kernel written in Bass

```python
import numpy as np
import jax
import jax.numpy as jnp

def _softmax(x, axis=-1):
    return jax.nn.softmax(x, axis=axis)

def _gelu(x):
    return jax.nn.gelu(x, approximate=True)

def _silu(x):
    return jax.nn.silu(x)

def _sigmoid(x):
    return jax.nn.sigmoid(x)

def _layernorm(x, axis=-1, eps=1e-05):
    m = jnp.mean(x, axis=axis, keepdims=True)
    v = jnp.var(x, axis=axis, keepdims=True)
    return (x - m) / jnp.sqrt(v + eps)

def _scatter_add(tgt, idx, src, axis=0):
    return tgt.at[idx].add(src)

def _segment_sum(src, seg, n):
    return jax.ops.segment_sum(src, seg, n)
kernel_name = 'mk_adj_preln_d2_adj_r2_f35004'

def setup_inputs(seed: int=0):
    np.random.seed(seed)
    _w = jnp.asarray

    def _rec_inputs():
        import jax
        import jax.numpy as jnp
        _gk = jax.random.key(seed)
        x = -0.0001538 + 1 * jax.random.normal(jax.random.fold_in(_gk, 1), (128, 64, 384), jnp.float32)
        _w = (1.0 + jnp.arange(64, dtype=jnp.float32)) ** (-0.5)
        _w = _w / _w.mean()
        _pij = jnp.clip(0.0625 * _w[:, None] * _w[None, :], 0.0, 1.0)
        _a = jax.random.uniform(jax.random.fold_in(_gk, 2), (128, 64, 64)) < _pij
        _af = _a.astype(jnp.float32)
        adj = _af
        return (x, adj)
    x, adj = _rec_inputs()

    def _L0_gnn_setup():
        import jax, jax.numpy as jnp
        import numpy as np
        LN_EPS = 1e-12

        def _digcn_forward(hidden_state, adjacency_matrix, Wl, bl, Ws, bs, Wr, br, ln_w, ln_b):
            B, S, D = hidden_state.shape
            temper = jnp.asarray(D, jnp.float32) ** 0.5
            i = jnp.arange(S)
            upper = (i[None, :] > i[:, None]).astype(hidden_state.dtype)
            lower = (i[None, :] < i[:, None]).astype(hidden_state.dtype)

            def layer(h, params):
                wl, b_l, ws, b_s, wr, b_r, g, beta = params
                u = jnp.einsum('bid,bjd->bij', h, h) / temper
                a = jax.nn.softmax(u, axis=-1)
                delta = a * adjacency_matrix
                attn = delta / (jnp.sum(delta, axis=-1, keepdims=True) + 1e-10)
                hl = h @ wl.T + b_l
                hs = h @ ws.T + b_s
                hr = h @ wr.T + b_r
                diag_a = jnp.diagonal(attn, axis1=1, axis2=2)
                ctx = jnp.einsum('bij,bjd->bid', attn * upper, hl) + diag_a[..., None] * hs + jnp.einsum('bij,bjd->bid', attn * lower, hr)
                mean = ctx.mean(-1, keepdims=True)
                var = ctx.var(-1, keepdims=True)
                o = (ctx - mean) / jnp.sqrt(var + LN_EPS) * g + beta
                return (jax.nn.relu(o), None)
            out, _ = jax.lax.scan(layer, hidden_state, (Wl, bl, Ws, bs, Wr, br, ln_w, ln_b))
            return out
        key = jax.random.key(seed)
        ks = jax.random.split(key, 6)
        B, S, D, L = (8, 512, 384, 2)
        scale = (1.0 / D) ** 0.5
        hidden_state = jax.random.normal(ks[0], (B, S, D), jnp.float32)
        adjacency_matrix = (jax.random.uniform(ks[1], (B, S, S)) < 0.05).astype(jnp.float32)
        Wl = jax.random.normal(ks[2], (L, D, D), jnp.float32) * scale
        Ws = jax.random.normal(ks[3], (L, D, D), jnp.float32) * scale
        Wr = jax.random.normal(ks[4], (L, D, D), jnp.float32) * scale
        bl = jnp.zeros((L, D), jnp.float32)
        bs = jnp.zeros((L, D), jnp.float32)
        br = jnp.zeros((L, D), jnp.float32)
        ln_w = jnp.ones((L, D), jnp.float32)
        ln_b = jnp.zeros((L, D), jnp.float32)
        return dict(hidden_state=hidden_state, adjacency_matrix=adjacency_matrix, Wl=Wl, bl=bl, Ws=Ws, bs=bs, Wr=Wr, br=br, ln_w=ln_w, ln_b=ln_b)
    _L0_gnn_all = _L0_gnn_setup()
    _L0_gnn_in = {k: v for k, v in _L0_gnn_all.items() if k in ('Wl', 'bl', 'Ws', 'bs', 'Wr', 'br', 'ln_w', 'ln_b')}
    del _L0_gnn_all

    def _L1_gnn_setup():
        import jax, jax.numpy as jnp
        import numpy as np
        B, L, H = (8, 1024, 384)
        LN_EPS = 1e-12
        key = jax.random.key(seed)
        ks = jax.random.split(key, 10)
        hidden_state = jax.random.normal(ks[0], (B, L, H), dtype=jnp.float32)
        adjacency = jax.random.randint(ks[1], (B, L, L), 0, 2).astype(jnp.float32)
        bound = 1.0 / np.sqrt(H)
        W_left = jax.random.normal(ks[2], (H, H), dtype=jnp.float32) * np.sqrt(2.0 / (H + H))
        b_left = jax.random.uniform(ks[3], (H,), minval=-bound, maxval=bound, dtype=jnp.float32)
        W_self = jax.random.normal(ks[4], (H, H), dtype=jnp.float32) * np.sqrt(2.0 / (H + H))
        b_self = jax.random.uniform(ks[5], (H,), minval=-bound, maxval=bound, dtype=jnp.float32)
        W_right = jax.random.normal(ks[6], (H, H), dtype=jnp.float32) * np.sqrt(2.0 / (H + H))
        b_right = jax.random.uniform(ks[7], (H,), minval=-bound, maxval=bound, dtype=jnp.float32)
        gamma = jnp.ones((H,), dtype=jnp.float32)
        beta = jnp.zeros((H,), dtype=jnp.float32)
        return {'hidden_state': hidden_state, 'adjacency': adjacency, 'W_left': W_left, 'b_left': b_left, 'W_self': W_self, 'b_self': b_self, 'W_right': W_right, 'b_right': b_right, 'gamma': gamma, 'beta': beta}
    _L1_gnn_all = _L1_gnn_setup()
    _L1_gnn_in = {k: v for k, v in _L1_gnn_all.items() if k in ('W_left', 'b_left', 'W_self', 'b_self', 'W_right', 'b_right', 'gamma', 'beta')}
    del _L1_gnn_all
    return {'x': x, 'adj': adj, 'L0_gnn_Wl': _L0_gnn_in['Wl'], 'L0_gnn_bl': _L0_gnn_in['bl'], 'L0_gnn_Ws': _L0_gnn_in['Ws'], 'L0_gnn_bs': _L0_gnn_in['bs'], 'L0_gnn_Wr': _L0_gnn_in['Wr'], 'L0_gnn_br': _L0_gnn_in['br'], 'L0_gnn_ln_w': _L0_gnn_in['ln_w'], 'L0_gnn_ln_b': _L0_gnn_in['ln_b'], 'L1_gnn_W_left': _L1_gnn_in['W_left'], 'L1_gnn_b_left': _L1_gnn_in['b_left'], 'L1_gnn_W_self': _L1_gnn_in['W_self'], 'L1_gnn_b_self': _L1_gnn_in['b_self'], 'L1_gnn_W_right': _L1_gnn_in['W_right'], 'L1_gnn_b_right': _L1_gnn_in['b_right'], 'L1_gnn_gamma': _L1_gnn_in['gamma'], 'L1_gnn_beta': _L1_gnn_in['beta']}

def reference(x, adj, L0_gnn_Wl, L0_gnn_bl, L0_gnn_Ws, L0_gnn_bs, L0_gnn_Wr, L0_gnn_br, L0_gnn_ln_w, L0_gnn_ln_b, L1_gnn_W_left, L1_gnn_b_left, L1_gnn_W_self, L1_gnn_b_self, L1_gnn_W_right, L1_gnn_b_right, L1_gnn_gamma, L1_gnn_beta):
    import jax
    import jax.numpy as jnp

    def _L0_gnn_ref(hidden_state, adjacency_matrix, Wl, bl, Ws, bs, Wr, br, ln_w, ln_b):
        import jax, jax.numpy as jnp
        import numpy as np
        LN_EPS = 1e-12

        def _digcn_forward(hidden_state, adjacency_matrix, Wl, bl, Ws, bs, Wr, br, ln_w, ln_b):
            B, S, D = hidden_state.shape
            temper = jnp.asarray(D, jnp.float32) ** 0.5
            i = jnp.arange(S)
            upper = (i[None, :] > i[:, None]).astype(hidden_state.dtype)
            lower = (i[None, :] < i[:, None]).astype(hidden_state.dtype)

            def layer(h, params):
                wl, b_l, ws, b_s, wr, b_r, g, beta = params
                u = jnp.einsum('bid,bjd->bij', h, h) / temper
                a = jax.nn.softmax(u, axis=-1)
                delta = a * adjacency_matrix
                attn = delta / (jnp.sum(delta, axis=-1, keepdims=True) + 1e-10)
                hl = h @ wl.T + b_l
                hs = h @ ws.T + b_s
                hr = h @ wr.T + b_r
                diag_a = jnp.diagonal(attn, axis1=1, axis2=2)
                ctx = jnp.einsum('bij,bjd->bid', attn * upper, hl) + diag_a[..., None] * hs + jnp.einsum('bij,bjd->bid', attn * lower, hr)
                mean = ctx.mean(-1, keepdims=True)
                var = ctx.var(-1, keepdims=True)
                o = (ctx - mean) / jnp.sqrt(var + LN_EPS) * g + beta
                return (jax.nn.relu(o), None)
            out, _ = jax.lax.scan(layer, hidden_state, (Wl, bl, Ws, bs, Wr, br, ln_w, ln_b))
            return out
        return _digcn_forward(hidden_state, adjacency_matrix, Wl, bl, Ws, bs, Wr, br, ln_w, ln_b)

    def _L1_gnn_ref(hidden_state, adjacency, W_left, b_left, W_self, b_self, W_right, b_right, gamma, beta):
        import jax, jax.numpy as jnp
        import numpy as np
        B, L, H = (8, 1024, 384)
        LN_EPS = 1e-12
        h = hidden_state
        d = h.shape[-1]
        n = h.shape[1]
        u = jnp.einsum('bld,bmd->blm', h, h) / jnp.sqrt(jnp.asarray(d, h.dtype))
        p = jax.nn.softmax(u, axis=-1)
        delta = p * adjacency
        attn = delta / (jnp.sum(delta, axis=2, keepdims=True) + 1e-10)
        h_left = jnp.einsum('bld,ed->ble', h, W_left) + b_left
        h_self = jnp.einsum('bld,ed->ble', h, W_self) + b_self
        h_right = jnp.einsum('bld,ed->ble', h, W_right) + b_right
        i = jnp.arange(n)[:, None]
        j = jnp.arange(n)[None, :]
        attn_left = jnp.where(j > i, attn, 0.0)
        attn_right = jnp.where(j < i, attn, 0.0)
        diag_a = jnp.diagonal(attn, axis1=1, axis2=2)
        ctx = jnp.einsum('blm,bmd->bld', attn_left, h_left) + diag_a[..., None] * h_self + jnp.einsum('blm,bmd->bld', attn_right, h_right)
        mu = jnp.mean(ctx, axis=-1, keepdims=True)
        var = jnp.mean(jnp.square(ctx - mu), axis=-1, keepdims=True)
        o = (ctx - mu) / jnp.sqrt(var + LN_EPS) * gamma + beta
        return jax.nn.relu(o)
    h = jnp.maximum(_layernorm(x, axis=-1), 0.0)
    x = x + _L0_gnn_ref(h, adj, L0_gnn_Wl, L0_gnn_bl, L0_gnn_Ws, L0_gnn_bs, L0_gnn_Wr, L0_gnn_br, L0_gnn_ln_w, L0_gnn_ln_b)
    h = jnp.maximum(_layernorm(x, axis=-1), 0.0)
    x = x + _L1_gnn_ref(h, adj, L1_gnn_W_left, L1_gnn_b_left, L1_gnn_W_self, L1_gnn_b_self, L1_gnn_W_right, L1_gnn_b_right, L1_gnn_gamma, L1_gnn_beta)
    return x

_drawn_inputs = setup_inputs


def setup_inputs(seed=0):
    import zlib

    import numpy as np

    out = dict(_drawn_inputs(seed))
    spreads = {'L0_gnn_bl': (0.0, 0.1),
     'L0_gnn_bs': (0.0, 0.1),
     'L0_gnn_br': (0.0, 0.1),
     'L0_gnn_ln_w': (1.0, 0.2),
     'L0_gnn_ln_b': (0.0, 0.1),
     'L1_gnn_gamma': (1.0, 0.2),
     'L1_gnn_beta': (0.0, 0.1)}
    factors = {'L1_gnn_b_left': 4.665, 'L1_gnn_b_self': 8.0, 'L1_gnn_b_right': 3.238}
    for name, (base, spread) in spreads.items():
        noise = np.random.default_rng([zlib.crc32(name.encode()), seed]).standard_normal(out[name].shape)
        drawn = base * np.exp(spread * noise) if base else spread * noise
        out[name] = jnp.asarray(drawn.astype(out[name].dtype))
    for name, factor in factors.items():
        out[name] = (out[name] * factor).astype(out[name].dtype)
    return out
```

```python
import concourse.bass as bass
from concourse import mybir
from contextlib import ExitStack

F32 = mybir.dt.float32
F32R = mybir.dt.float32r
ALU = mybir.AluOpType
ACT = mybir.ActivationFunctionType
AX = mybir.AxisListType

P = 128
NODES = 64
D = 384
CH = D // P
TILES = 64
PAIRS = TILES // 2
PHASES = 3
STEPS = PHASES * PAIRS
SCALE = float(D) ** -0.5
LN_EPS = 1e-5
GNN_EPS = 1e-12
GUARD = 1e-10
HI, LO = 0, 1
LEFT, RIGHT, SELF = 0, 1, 2
ROW_GAMMA, ROW_BETA, ROW_LEFT, ROW_RIGHT, ROW_SELF = range(5)
PIECES = 3 * CH + 1
HALVES = (slice(0, NODES), slice(NODES, P))


class Step:

    def __init__(self, phase, half, parity):
        self.half, self.parity = half, parity
        self.n = 2 * half + parity
        self.phase = self.n // PAIRS if isinstance(half, int) else phase
        self.g = self.n - PAIRS * self.phase
        self.normal = self.n - (PAIRS if self.phase == 2 else 0)

    def ahead(self, k):
        parity = self.parity + k
        return Step(self.phase, self.half + parity // 2, parity % 2)

    def exists(self):
        return not isinstance(self.n, int) or 0 <= self.n < STEPS

    def tile(self, k):
        return 2 * self.n + k

    def slot(self, k):
        return bass.ds(2 * self.g + k, 1)


def at_least(eng, sem, value):
    if not isinstance(value, int) or value > 0:
        eng.wait_ge(sem, value)


def walk(eng, body):
    for phase in range(PHASES):
        first, last = phase * PAIRS // 2, (phase + 1) * PAIRS // 2 - 1
        body(Step(phase, first, 0))
        body(Step(phase, first, 1))
        with eng.Fori(first + 1, last) as half:
            body(Step(phase, half, 0))
            body(Step(phase, half, 1))
        body(Step(phase, last, 0))
        body(Step(phase, last, 1))


def adj_gnn_program(nc, x, adj, weights, vectors, identity, triangles, out):
    x_pairs = x.rearrange("(g k p) d -> g p k d", k=2, p=P)
    out_pairs = out.rearrange("(g k p) d -> g p k d", k=2, p=P)

    ctx = ExitStack()
    with ctx:
        def sb(name, shape, dt=F32):
            return ctx.enter_context(nc.sbuf_tensor(name, shape, dt))

        def bank(name):
            return ctx.enter_context(nc.psum_tensor(name, [P, 512], F32))

        def sem(name):
            return ctx.enter_context(nc.semaphore(name))

        rows = sb("rows", [P, TILES, D])
        weight = sb("weight", [P, 2, 3, CH, 2, D], F32R)
        piece = sb("piece", [P, 2, D])
        vector_rows = sb("vector_rows", [P, 4, D])
        self_bias = sb("self_bias", [P, 2, D], F32R)
        one_64th = sb("one_64th", [P, P], F32R)
        ident = sb("ident", [P, P])
        tri = sb("tri", [P, 3, NODES])
        source = sb("source", [P, 2, D])
        node_t = sb("node_t", [P, 2, 2, CH, 2, P], F32R)
        side_rows = sb("side_rows", [P, 2, D])
        side_parts = sb("side_parts", [P, 2, 2, D], F32R)
        cross = sb("cross", [P, 2, NODES])
        score = sb("score", [P, 2, NODES])
        prob = sb("prob", [P, 2, NODES])
        edge = sb("edge", [P, 2, NODES])
        edge3 = sb("edge3", [P, 2, 3, NODES])
        edge_block = sb("edge_block", [P, 2, 2, P])
        attn_t = sb("attn_t", [P, 2, 2, 2, P], F32R)
        adj_in = sb("adj_in", [P, 2, 2, NODES])
        context = sb("context", [P, 2, D])
        io = sb("io", [P, 2, 2, D])
        row_max = sb("row_max", [P, 2])
        total = sb("total", [P, 2, 2])
        kept = sb("kept", [P, 2])
        diag = sb("diag", [P, 2, 2])
        den = sb("den", [P, 2])
        den_sq = sb("den_sq", [P, 2, 2])
        stats = sb("stats", [P, 2, 6])
        moments = sb("moments", [P, 2, 2])
        spread = sb("spread", [P, 2])
        rstd = sb("rstd", [P, 2])
        in_stats = sb("in_stats", [P, 2, 6])
        in_moments = sb("in_moments", [P, 2, 2])
        in_spread = sb("in_spread", [P, 2])
        in_rstd = sb("in_rstd", [P, 2])
        in_shift = sb("in_shift", [P, 2])
        scalars = sb("scalars", [P, 5])
        minus_half, ln_eps, gate = scalars[:, 0:2], scalars[:, 2:4], scalars[:, 4:5]

        side_bank = [bank("left_bank"), bank("right_bank")]
        self_bank = bank("self_bank")
        context_bank = bank("context_bank")
        node_bank = bank("node_bank")
        score_bank = bank("score_bank")
        edge_bank = bank("edge_bank")
        scores4 = score_bank[:, :].rearrange("p (k a j) -> p k a j", k=2, a=2)
        node_3 = node_bank[:, 0:D].rearrange("p (c r) -> p c r", c=CH)

        constants_in = sem("constants_in")
        piece_in = [sem("piece_in0"), sem("piece_in1")]
        side_rows_in = sem("side_rows_in")
        norm_rows_in = sem("norm_rows_in")
        x_in = [sem("x_in0"), sem("x_in1")]
        residual_in = [sem("residual_in0"), sem("residual_in1")]
        adj_arrived = [sem("adj_arrived0"), sem("adj_arrived1")]
        out_written = [sem("out_written0"), sem("out_written1")]
        consts_set = sem("consts_set")
        piece_hi = sem("piece_hi")
        piece_lo = sem("piece_lo")
        in_stats_done = sem("in_stats_done")
        in_stats_raw = sem("in_stats_raw")
        in_spread_done = sem("in_spread_done")
        in_rstd_done = sem("in_rstd_done")
        in_shift_done = sem("in_shift_done")
        source_ready = sem("source_ready")
        node_moved = sem("node_moved")
        node_hi = sem("node_hi")
        node_lo = sem("node_lo")
        scored = sem("scored")
        cross_copied = sem("cross_copied")
        score_summed = sem("score_summed")
        max_done = sem("max_done")
        shift_done = sem("shift_done")
        exp_done = sem("exp_done")
        edge_done = sem("edge_done")
        edge3_done = sem("edge3_done")
        kept_done = sem("kept_done")
        diag_done = sem("diag_done")
        den_done = sem("den_done")
        den_sq_done = sem("den_sq_done")
        blocks_placed = sem("blocks_placed")
        edges_moved = sem("edges_moved")
        attn_hi = sem("attn_hi")
        attn_lo = sem("attn_lo")
        side_product = [sem("left_product"), sem("right_product")]
        side_biased = [sem("left_biased"), sem("right_biased")]
        side_hi = [sem("left_hi"), sem("right_hi")]
        side_lo = [sem("left_lo"), sem("right_lo")]
        self_product = sem("self_product")
        self_scaled = sem("self_scaled")
        context_product = sem("context_product")
        context_done = sem("context_done")
        stats_done = sem("stats_done")
        moments_done = sem("moments_done")
        spread_done = sem("spread_done")
        rstd_done = sem("rstd_done")
        centred = sem("centred")
        normed = sem("normed")
        post_done = sem("post_done")

        block = ctx.enter_context(nc.Block())

        @block.sync
        def _(sp):
            def load_x(s):
                at_least(sp, in_stats_done, 2 * s.n - 2)
                sp.dma_start(rows[:, bass.ds(2 * s.g, 2), :],
                             x_pairs[bass.ds(s.g, 1)].rearrange("g p k d -> p (g k) d")).then_inc(x_in[s.parity], 16)

            def load_residual(s):
                at_least(sp, post_done, s.tile(0) - 2)
                sp.dma_start(io[:, s.parity], x_pairs[bass.ds(s.g, 1)].rearrange("g p k d -> p (g k) d"))\
                  .then_inc(residual_in[s.parity], 16)

            def load_adj(s):
                at_least(sp, edge_done, s.n - 1)
                sp.dma_start(adj_in[:, s.parity], adj[:, bass.ds(2 * s.g, 2), :]).then_inc(adj_arrived[s.parity], 16)

            def load_piece(phase, i):
                n = phase * PIECES + i
                at_least(sp, piece_lo, n - 1)
                src = weights[phase, i] if i < 3 * CH else vectors[phase, ROW_SELF].partition_broadcast(P)
                sp.dma_start(piece[:, n % 2], src).then_inc(piece_in[n % 2], 16)

            def load_side_rows(phase):
                for side in (LEFT, RIGHT):
                    at_least(sp, side_biased[side], 2 * PAIRS * phase)
                    sp.dma_start(vector_rows[:, ROW_LEFT + side], vectors[phase, ROW_LEFT + side].partition_broadcast(P))\
                      .then_inc(side_rows_in, 16)

            def load_norm_rows(phase):
                at_least(sp, post_done, 2 * PAIRS * phase)
                for v in (ROW_GAMMA, ROW_BETA):
                    sp.dma_start(vector_rows[:, v], vectors[phase, v].partition_broadcast(P)).then_inc(norm_rows_in, 16)

            def store(s):
                at_least(sp, post_done, s.tile(2))
                sp.dma_start(out_pairs[bass.ds(s.g, 1)].rearrange("g p k d -> p (g k) d"), io[:, s.parity])\
                  .then_inc(out_written[s.parity], 16)

            def body(s):
                prev, nxt, after = s.ahead(-1), s.ahead(1), s.ahead(2)
                if isinstance(s.n, int) and s.g == 0 and s.phase > 0:
                    load_side_rows(s.phase)
                if after.exists() and after.phase == 0:
                    load_x(after)
                if after.exists():
                    load_adj(after)
                if nxt.exists() and nxt.phase == 1:
                    load_residual(nxt)
                if isinstance(s.n, int) and s.g == 0 and s.phase > 0:
                    load_norm_rows(s.phase)
                if prev.exists() and prev.phase == 2:
                    store(prev)
                if isinstance(s.n, int) and s.g >= PAIRS - 2 and s.phase + 1 < PHASES:
                    for i in range(PIECES // 2):
                        load_piece(s.phase + 1, (s.g - PAIRS + 2) * (PIECES // 2) + i)

            load_x(Step(0, 0, 0))
            sp.dma_start(ident[:, :], identity).then_inc(constants_in, 16)
            load_piece(0, 0)
            load_adj(Step(0, 0, 0))
            sp.dma_start(tri[:, :, :], triangles).then_inc(constants_in, 16)
            load_piece(0, 1)
            load_x(Step(0, 0, 1))
            load_side_rows(0)
            load_adj(Step(0, 0, 1))
            for i in range(2, PIECES):
                load_piece(0, i)
            load_norm_rows(0)
            walk(sp, body)
            store(Step(2, STEPS // 2 - 1, 1))
            for parity in range(2):
                sp.wait_ge(out_written[parity], 16 * PAIRS // 2)

        @block.tensor
        def _(pe):
            def transpose_nodes(s, k):
                pe.wait_ge(source_ready, s.tile(k) + 1)
                at_least(pe, node_lo, s.tile(k))
                for c in range(CH):
                    mm = nc.tensor.transpose(node_bank[:, c * P:(c + 1) * P], source[:, k, c * P:(c + 1) * P], ident[:, :])
                mm.then_inc(node_moved, 1)

            def scores(s):
                pe.wait_ge(node_hi, s.tile(2))
                pe.wait_ge(node_lo, s.tile(2))
                at_least(pe, score_summed, 2 * s.n)
                for k in range(2):
                    for c in range(CH):
                        t = node_t[:, s.parity, k, c].rearrange("p a r -> p (a r)")
                        nc.tensor.matmul(score_bank[:, k * 256:(k + 1) * 256], t[:, 0:P], t,
                                         start=(c == 0), stop=False, skip_group_check=True)
                        mm = nc.tensor.matmul(score_bank[:, k * 256:k * 256 + P], t[:, P:2 * P], t[:, 0:P],
                                              start=False, stop=(c == CH - 1), skip_group_check=True)
                mm.then_inc(scored, 1)

            def transpose_edges(s):
                pe.wait_ge(blocks_placed, 2 * s.n + 2)
                at_least(pe, attn_lo, s.n)
                for k in range(2):
                    for ul in range(2):
                        at = (2 * k + ul) * P
                        mm = nc.tensor.transpose(edge_bank[:, at:at + P], edge_block[:, k, ul], ident[:, :])
                mm.then_inc(edges_moved, 1)

            def project(s, k, w, bank, done):
                for c in range(CH):
                    for a, b in ((HI, HI), (HI, LO), (LO, HI)):
                        last = w != SELF and (c, a) == (CH - 1, LO)
                        mm = nc.tensor.matmul(bank[:, 0:D], node_t[:, s.parity, k, c, a], weight[:, s.phase % 2, w, c, b],
                                              start=(c == 0 and a == b), stop=last)
                if w == SELF:
                    mm = nc.tensor.matmul(bank[:, 0:D], one_64th[:, :], self_bias[:, s.phase % 2], start=False, stop=True)
                mm.then_inc(done, 1)

            def project_side(s, k, side):
                if side == LEFT:
                    pe.wait_ge(node_hi, s.tile(k) + 1)
                    pe.wait_ge(node_lo, s.tile(k) + 1)
                at_least(pe, side_biased[side], s.tile(k))
                project(s, k, side, side_bank[side], side_product[side])

            def project_self(s, k):
                at_least(pe, self_scaled, s.tile(k))
                project(s, k, SELF, self_bank, self_product)

            def weigh(s, k):
                pe.wait_ge(attn_hi, s.n + 1)
                pe.wait_ge(attn_lo, s.n + 1)
                at_least(pe, context_done, s.tile(k))
                for side in (LEFT, RIGHT):
                    pe.wait_ge(side_hi[side], s.tile(k) + 1)
                    pe.wait_ge(side_lo[side], s.tile(k) + 1)
                    for a, b in ((HI, HI), (HI, LO), (LO, HI)):
                        mm = nc.tensor.matmul(context_bank[:, 0:D], attn_t[:, a, k, side], side_parts[:, side, b],
                                              start=(side == LEFT and a == b), stop=(side == RIGHT and a == LO))
                mm.then_inc(context_product, 1)

            def body(s):
                nxt = s.ahead(1)
                if isinstance(s.n, int) and s.g == 0:
                    pe.wait_ge(piece_lo, (s.phase + 1) * PIECES)
                project_side(s, 0, LEFT)
                transpose_edges(s)
                if nxt.exists():
                    transpose_nodes(nxt, 0)
                project_side(s, 0, RIGHT)
                if nxt.exists():
                    transpose_nodes(nxt, 1)
                project_self(s, 0)
                weigh(s, 0)
                if nxt.exists():
                    scores(nxt)
                project_side(s, 1, LEFT)
                project_side(s, 1, RIGHT)
                project_self(s, 1)
                weigh(s, 1)

            pe.wait_ge(constants_in, 32)
            pe.wait_ge(consts_set, 1)
            start = Step(0, 0, 0)
            transpose_nodes(start, 0)
            transpose_nodes(start, 1)
            scores(start)
            walk(pe, body)

        @block.scalar
        def _(act):
            def fill_source(s, k):
                at_least(act, node_moved, s.tile(k) - 1)
                if s.phase == 1:
                    nc.scalar.activation(source[:, k:k + 1], rows[:, s.slot(k)], ACT.Copy).then_inc(source_ready, 1)
                else:
                    act.wait_ge(in_shift_done, s.normal + 1)
                    nc.scalar.activation(source[:, k:k + 1], rows[:, s.slot(k)], ACT.Identity, bias=in_shift[:, k:k + 1],
                                         scale=in_rstd[:, k:k + 1]).then_inc(source_ready, 1)

            def split_nodes(s, k):
                act.wait_ge(node_moved, s.tile(k) + 1)
                nc.scalar.activation(node_t[:, s.parity, k, :, HI], node_3, ACT.Relu).then_inc(node_hi, 1)

            def copy_cross(s):
                act.wait_ge(scored, s.n + 1)
                at_least(act, score_summed, 2 * s.n)
                for h, half in enumerate(HALVES):
                    nc.scalar.activation(cross[half], scores4[half, :, 1, h * NODES:(h + 1) * NODES], ACT.Copy)\
                      .then_inc(cross_copied, 1)

            def exponentials(s):
                act.wait_ge(shift_done, s.n + 1)
                at_least(act, edge_done, s.n)
                for k in range(2):
                    nc.scalar.activation(prob[:, k], score[:, k], ACT.Exp, scale=SCALE,
                                         accum_out=total[:, s.parity, k:k + 1]).then_inc(exp_done, 1)

            def place_blocks(s):
                act.wait_ge(edge3_done, s.n + 1)
                at_least(act, edges_moved, s.n)
                for h, half in enumerate(HALVES):
                    nc.scalar.activation(edge_block[half, :, :, h * NODES:(h + 1) * NODES], edge3[half, :, 0:2], ACT.Copy)\
                      .then_inc(blocks_placed, 1)

            def split_edges(s):
                act.wait_ge(edges_moved, s.n + 1)
                nc.scalar.activation(attn_t[:, HI].rearrange("p k u r -> p (k u r)"), edge_bank[:, :], ACT.Copy).then_inc(attn_hi, 1)

            def split_side(s, k, side):
                act.wait_ge(side_biased[side], s.tile(k) + 1)
                nc.scalar.activation(side_parts[:, side, HI], side_rows[:, side], ACT.Copy).then_inc(side_hi[side], 1)

            def scale_self(s, k):
                act.wait_ge(self_product, s.tile(k) + 1)
                act.wait_ge(diag_done, s.n + 1)
                at_least(act, post_done, s.tile(k) - 1)
                nc.scalar.activation(context[:, k], self_bank[:, 0:D], ACT.Identity,
                                     scale=diag[:, s.parity, k:k + 1]).then_inc(self_scaled, 1)

            def split_piece(phase, i):
                n = phase * PIECES + i
                act.wait_ge(piece_in[n % 2], 16 * (n // 2 + 1))
                to = weight[:, phase % 2, i // CH, i % CH, HI] if i < 3 * CH else self_bias[:, phase % 2]
                nc.scalar.activation(to, piece[:, n % 2], ACT.Copy).then_inc(piece_hi, 1)

            def body(s):
                nxt, after = s.ahead(1), s.ahead(2)
                split_side(s, 0, LEFT)
                split_edges(s)
                if nxt.exists():
                    split_nodes(nxt, 0)
                split_side(s, 0, RIGHT)
                if nxt.exists():
                    split_nodes(nxt, 1)
                scale_self(s, 0)
                if nxt.exists():
                    copy_cross(nxt)
                    exponentials(nxt)
                split_side(s, 1, LEFT)
                if nxt.exists():
                    place_blocks(nxt)
                split_side(s, 1, RIGHT)
                if after.exists():
                    fill_source(after, 0)
                scale_self(s, 1)
                if after.exists():
                    fill_source(after, 1)
                if isinstance(s.n, int) and s.g >= PAIRS - 2 and s.phase + 1 < PHASES:
                    for i in range(PIECES // 2):
                        split_piece(s.phase + 1, (s.g - PAIRS + 2) * (PIECES // 2) + i)

            start = Step(0, 0, 0)
            fill_source(start, 0)
            fill_source(start, 1)
            act.wait_ge(consts_set, 1)
            split_nodes(start, 0)
            split_nodes(start, 1)
            split_piece(0, 0)
            split_piece(0, 1)
            copy_cross(start)
            exponentials(start)
            place_blocks(start)
            for i in range(2, PIECES):
                split_piece(0, i)
            fill_source(start.ahead(1), 0)
            fill_source(start.ahead(1), 1)
            walk(act, body)

        @block.vector
        def _(dve):
            def input_stats(s, k):
                if s.phase == 0:
                    dve.wait_ge(x_in[s.parity], 16 * (s.half + 1))
                at_least(dve, in_rstd_done, s.normal)
                nc.vector.bn_stats(in_stats[:, k], rows[:, s.slot(k)]).then_inc(in_stats_raw, 1)
                dve.wait_ge(in_stats_raw, 2 * s.normal + k + 1)
                nc.vector.memset(gate[:, :], 0.0)
                nc.vector.bn_aggr(in_moments[:, k], in_stats[:, k]).then_inc(in_stats_done, 1)

            def input_shift(s):
                dve.wait_ge(in_rstd_done, s.normal + 1)
                at_least(dve, source_ready, s.tile(0))
                nc.vector.scalar_tensor_tensor(in_shift[:, :], in_moments[:, :, 0], -1.0, in_rstd[:, :],
                                               ALU.mult, ALU.mult).then_inc(in_shift_done, 1)

            def split_nodes(s, k):
                dve.wait_ge(node_hi, s.tile(k) + 1)
                nc.vector.scalar_tensor_tensor(node_t[:, s.parity, k, :, LO], node_3, 0.0,
                                               node_t[:, s.parity, k, :, HI].bitcast(F32),
                                               ALU.max, ALU.subtract).then_inc(node_lo, 1)

            def shift_scores(s):
                dve.wait_ge(cross_copied, 2 * s.n + 2)
                at_least(dve, exp_done, 2 * s.n)
                for h, half in enumerate(HALVES):
                    nc.vector.tensor_tensor(score[half], scores4[half, :, 0, h * NODES:(h + 1) * NODES], cross[half],
                                            ALU.add).then_inc(score_summed, 1)
                dve.wait_ge(score_summed, 2 * s.n + 2)
                nc.vector.tensor_reduce(row_max[:, :], score[:, :, :], op=ALU.max, axis=AX.X).then_inc(max_done, 1)
                dve.wait_ge(max_done, s.n + 1)
                nc.vector.tensor_tensor(score[:, :, :], score[:, :, :],
                                        row_max[:, :].unsqueeze(2).to_broadcast([P, 2, NODES]),
                                        ALU.subtract).then_inc(shift_done, 1)

            def edges(s):
                dve.wait_ge(exp_done, 2 * s.n + 2)
                dve.wait_ge(adj_arrived[s.parity], 16 * (s.half + 1))
                at_least(dve, edge3_done, s.n)
                nc.vector.tensor_tensor(edge[:, :, :], prob[:, :, :], adj_in[:, s.parity], ALU.mult).then_inc(edge_done, 1)
                dve.wait_ge(edge_done, s.n + 1)
                nc.vector.tensor_reduce(kept[:, :], edge[:, :, :], op=ALU.add, axis=AX.X).then_inc(kept_done, 1)
                dve.wait_ge(kept_done, s.n + 1)
                nc.vector.scalar_tensor_tensor(den[:, :], total[:, s.parity], GUARD, kept[:, :],
                                               ALU.mult, ALU.add).then_inc(den_done, 1)

            def diagonal(s):
                dve.wait_ge(edge3_done, s.n + 1)
                nc.vector.tensor_reduce(diag[:, s.parity], edge3[:, :, 2], op=ALU.add, axis=AX.X).then_inc(diag_done, 1)
                dve.wait_ge(den_done, s.n + 1)
                nc.vector.tensor_tensor(den_sq[:, s.parity], den[:, :], den[:, :], ALU.mult).then_inc(den_sq_done, 1)

            def split_edges(s):
                dve.wait_ge(attn_hi, s.n + 1)
                nc.vector.tensor_tensor(attn_t[:, LO].rearrange("p k u r -> p (k u r)"), edge_bank[:, :],
                                        attn_t[:, HI].rearrange("p k u r -> p (k u r)").bitcast(F32),
                                        ALU.subtract).then_inc(attn_lo, 1)

            def add_bias(s, k, side):
                dve.wait_ge(side_product[side], s.tile(k) + 1)
                at_least(dve, side_lo[side], s.tile(k))
                if isinstance(s.n, int) and s.g == 0:
                    dve.wait_ge(side_rows_in, 32 * (s.phase + 1))
                nc.vector.tensor_tensor(side_rows[:, side], side_bank[side][:, 0:D], vector_rows[:, ROW_LEFT + side],
                                        ALU.add).then_inc(side_biased[side], 1)

            def sum_context(s, k):
                dve.wait_ge(context_product, s.tile(k) + 1)
                dve.wait_ge(self_scaled, s.tile(k) + 1)
                nc.vector.tensor_tensor(context[:, k], context_bank[:, 0:D], context[:, k], ALU.add).then_inc(context_done, 1)
                dve.wait_ge(context_done, s.tile(k) + 1)
                nc.vector.bn_stats(stats[:, k], context[:, k]).then_inc(stats_done, 1)
                dve.wait_ge(stats_done, s.tile(k) + 1)
                nc.vector.memset(gate[:, :], 0.0)
                nc.vector.bn_aggr(moments[:, k], stats[:, k]).then_inc(moments_done, 1)

            def spreads(s):
                dve.wait_ge(moments_done, s.tile(2))
                dve.wait_ge(den_sq_done, s.n + 1)
                nc.vector.scalar_tensor_tensor(spread[:, :], den_sq[:, s.parity], GNN_EPS, moments[:, :, 1],
                                               ALU.mult, ALU.add).then_inc(spread_done, 1)

            def centre(s, k):
                if isinstance(s.n, int) and s.g == 0:
                    dve.wait_ge(norm_rows_in, 32 * (s.phase + 1))
                dve.wait_ge(moments_done, s.tile(k) + 1)
                nc.vector.scalar_tensor_tensor(context[:, k], context[:, k], moments[:, k, 0:1], vector_rows[:, ROW_GAMMA],
                                               ALU.subtract, ALU.mult).then_inc(centred, 1)

            def norm(s, k):
                dve.wait_ge(rstd_done, s.n + 1)
                dve.wait_ge(centred, s.tile(k) + 1)
                to, done = (rows[:, s.slot(k)], post_done) if s.phase == 0 else (context[:, k:k + 1], normed)
                nc.vector.scalar_tensor_tensor(to, context[:, k:k + 1], rstd[:, k:k + 1], vector_rows[:, ROW_BETA:ROW_BETA + 1],
                                               ALU.mult, ALU.add).then_inc(done, 1)

            def residual(s, k):
                dve.wait_ge(normed, s.tile(k) + 1 - 2 * PAIRS)
                if s.phase == 1:
                    dve.wait_ge(residual_in[s.parity], 16 * (s.half + 1 - PAIRS // 2))
                    other, to = io[:, s.parity, k:k + 1], rows[:, s.slot(k)]
                else:
                    at_least(dve, out_written[s.parity], 16 * (s.half - PAIRS))
                    other, to = rows[:, s.slot(k)], io[:, s.parity, k:k + 1]
                nc.vector.scalar_tensor_tensor(to, context[:, k:k + 1], 0.0, other, ALU.max, ALU.add).then_inc(post_done, 1)

            def body(s):
                prev, nxt, after = s.ahead(-1), s.ahead(1), s.ahead(2)
                if prev.exists():
                    sum_context(prev, 1)
                    spreads(prev)
                add_bias(s, 0, LEFT)
                split_edges(s)
                if nxt.exists():
                    split_nodes(nxt, 0)
                if prev.exists():
                    centre(prev, 0)
                add_bias(s, 0, RIGHT)
                if nxt.exists():
                    split_nodes(nxt, 1)
                if prev.exists():
                    norm(prev, 0)
                    if prev.phase > 0:
                        residual(prev, 0)
                    centre(prev, 1)
                    norm(prev, 1)
                sum_context(s, 0)
                if nxt.exists():
                    shift_scores(nxt)
                if after.exists() and after.phase != 1:
                    input_stats(after, 0)
                add_bias(s, 1, LEFT)
                if nxt.exists():
                    edges(nxt)
                if after.exists() and after.phase != 1:
                    input_stats(after, 1)
                if prev.exists() and prev.phase > 0:
                    residual(prev, 1)
                add_bias(s, 1, RIGHT)
                if nxt.exists():
                    diagonal(nxt)
                if after.exists() and after.phase != 1:
                    input_shift(after)

            start = Step(0, 0, 0)
            nc.vector.memset(edge_block[:, :, :, :], 0.0)
            nc.vector.memset(minus_half[:, :], -0.5)
            nc.vector.memset(ln_eps[:, :], LN_EPS)
            nc.vector.memset(one_64th[:, :].bitcast(F32), 1.0 / 64).then_inc(consts_set, 1)
            input_stats(start, 0)
            input_stats(start, 1)
            input_shift(start)
            split_nodes(start, 0)
            split_nodes(start, 1)
            shift_scores(start)
            edges(start)
            diagonal(start)
            for k in range(2):
                input_stats(start.ahead(1), k)
            input_shift(start.ahead(1))
            walk(dve, body)
            final = Step(2, STEPS // 2 - 1, 1)
            sum_context(final, 1)
            spreads(final)
            for k in range(2):
                centre(final, k)
                norm(final, k)
                residual(final, k)

        @block.gpsimd
        def _(pool):
            def input_rstd(s):
                pool.wait_ge(in_stats_done, 2 * s.normal + 2)
                at_least(pool, source_ready, s.tile(0))
                nc.gpsimd.tensor_tensor(in_spread[:, :], in_moments[:, :, 1], ln_eps[:, :], ALU.add).then_inc(in_spread_done, 1)
                pool.wait_ge(in_spread_done, s.normal + 1)
                nc.gpsimd.tensor_tensor(in_rstd[:, :], in_spread[:, :], minus_half[:, :], ALU.pow).then_inc(in_rstd_done, 1)

            def output_rstd(s):
                pool.wait_ge(spread_done, s.n + 1)
                nc.gpsimd.tensor_tensor(rstd[:, :], spread[:, :], minus_half[:, :], ALU.pow).then_inc(rstd_done, 1)

            def split_side(s, k, side):
                pool.wait_ge(side_hi[side], s.tile(k) + 1)
                nc.gpsimd.tensor_tensor(side_parts[:, side, LO], side_rows[:, side], side_parts[:, side, HI].bitcast(F32),
                                        ALU.subtract).then_inc(side_lo[side], 1)

            def triangles_of(s):
                pool.wait_ge(edge_done, s.n + 1)
                at_least(pool, blocks_placed, 2 * s.n)
                at_least(pool, diag_done, s.n)
                nc.gpsimd.tensor_tensor(edge3[:, :, :, :], edge[:, :, :].unsqueeze(2).to_broadcast([P, 2, 3, NODES]),
                                        tri[:, :, :].unsqueeze(1).to_broadcast([P, 2, 3, NODES]), ALU.mult).then_inc(edge3_done, 1)

            def split_piece(phase, i):
                n = phase * PIECES + i
                pool.wait_ge(piece_hi, n + 1)
                if i < 3 * CH:
                    to, hi, raw = weight[:, phase % 2, i // CH, i % CH, LO], weight[:, phase % 2, i // CH, i % CH, HI], piece[:, n % 2]
                else:
                    low = HALVES[1]
                    to, hi, raw = self_bias[low, phase % 2], self_bias[low, phase % 2], piece[low, n % 2]
                if i == 3 * CH:
                    pool.wait_ge(piece_lo, n)
                nc.gpsimd.tensor_tensor(to, raw, hi.bitcast(F32), ALU.subtract).then_inc(piece_lo, 1)
                if i == 3 * CH:
                    pool.wait_ge(piece_lo, n + 1)

            def body(s):
                prev, nxt, after = s.ahead(-1), s.ahead(1), s.ahead(2)
                if prev.exists():
                    output_rstd(prev)
                split_side(s, 0, LEFT)
                split_side(s, 0, RIGHT)
                if nxt.exists():
                    triangles_of(nxt)
                split_side(s, 1, LEFT)
                if after.exists() and after.phase != 1:
                    input_rstd(after)
                split_side(s, 1, RIGHT)
                if isinstance(s.n, int) and s.g >= PAIRS - 2 and s.phase + 1 < PHASES:
                    for i in range(PIECES // 2):
                        split_piece(s.phase + 1, (s.g - PAIRS + 2) * (PIECES // 2) + i)

            pool.wait_ge(constants_in, 32)
            pool.wait_ge(consts_set, 1)
            start = Step(0, 0, 0)
            input_rstd(start)
            split_piece(0, 0)
            split_piece(0, 1)
            triangles_of(start)
            for i in range(2, PIECES):
                split_piece(0, i)
            input_rstd(start.ahead(1))
            walk(pool, body)
            output_rstd(Step(2, STEPS // 2 - 1, 1))


def kernel(**inputs):
    import numpy as np
    import concourse.bacc as bacc
    from concourse.bass_utils import run_bass_kernel_spmd

    given = {name: np.asarray(value) for name, value in inputs.items()}

    def layer(kind, name):
        return [given["L0_gnn_" + kind[0]][0], given["L0_gnn_" + kind[0]][1], given["L1_gnn_" + kind[1]]][name]

    matrices = [[layer(kind, n) for kind in (("Wl", "W_left"), ("Wr", "W_right"), ("Ws", "W_self"))] for n in range(PHASES)]
    rows = [[layer(kind, n) for kind in (("ln_w", "gamma"), ("ln_b", "beta"), ("bl", "b_left"), ("br", "b_right"), ("bs", "b_self"))]
            for n in range(PHASES)]
    below = np.tril(np.ones((NODES, NODES), np.float32), -1)
    triangles = np.stack([below.T, below, np.eye(NODES, dtype=np.float32)], axis=1)
    arrays = {
        "x": np.ascontiguousarray(given["x"].reshape(TILES * P, D)),
        "adj": np.ascontiguousarray(given["adj"].reshape(TILES, P, NODES).transpose(1, 0, 2)),
        "weights": np.ascontiguousarray(np.stack([np.stack([m.T.reshape(CH, P, D) for m in ms]) for ms in matrices])
                                        .reshape(PHASES, 3 * CH, P, D)),
        "vectors": np.ascontiguousarray(np.stack([np.stack(r) for r in rows])),
        "identity": np.eye(P, dtype=np.float32),
        "triangles": np.concatenate([triangles, triangles]),
    }
    nc = bacc.Bacc("TRN2", target_bir_lowering=False, num_devices=1)
    aps = [nc.dram_tensor(name, a.shape, mybir.dt.from_np(a.dtype), kind="ExternalInput").ap() for name, a in arrays.items()]
    out = nc.dram_tensor("out", (TILES * P, D), F32, kind="ExternalOutput").ap()
    adj_gnn_program(nc, *aps, out)
    result = run_bass_kernel_spmd(nc, [arrays], core_ids=[0])
    return result.results[0]["out"].reshape(TILES * P // NODES, NODES, D)
```

```python
import concourse.bass as bass
from concourse import mybir
from contextlib import ExitStack

F32 = mybir.dt.float32
F32R = mybir.dt.float32r
ALU = mybir.AluOpType
ACT = mybir.ActivationFunctionType
AX = mybir.AxisListType

P = 128
NODES = 64
D = 384
CH = D // P
TILES = 64
PAIRS = TILES // 2
PHASES = 3
STEPS = PHASES * PAIRS
SCALE = float(D) ** -0.5
LN_EPS = 1e-5
GNN_EPS = 1e-12
GUARD = 1e-10
HI, LO = 0, 1
LEFT, RIGHT, SELF = 0, 1, 2
ROW_GAMMA, ROW_BETA, ROW_LEFT, ROW_RIGHT, ROW_SELF = range(5)
PIECES = 3 * CH + 1
HALVES = (slice(0, NODES), slice(NODES, P))


class Step:

    def __init__(self, phase, half, parity):
        self.half, self.parity = half, parity
        self.n = 2 * half + parity
        self.phase = self.n // PAIRS if isinstance(half, int) else phase
        self.g = self.n - PAIRS * self.phase
        self.bounded = self.phase != 1
        self.normal = self.n - (PAIRS if self.phase == 2 else 0)

    def before_bounded(self):
        return self.normal if self.bounded else PAIRS

    def ahead(self, k):
        parity = self.parity + k
        return Step(self.phase, self.half + parity // 2, parity % 2)

    def exists(self):
        return not isinstance(self.n, int) or 0 <= self.n < STEPS

    def tile(self, k):
        return 2 * self.n + k

    def slot(self, k):
        return bass.ds(2 * self.g + k, 1)


def is_first(s):
    return isinstance(s.n, int) and s.n == 0


def at_least(eng, sem, value):
    if not isinstance(value, int) or value > 0:
        eng.wait_ge(sem, value)


PIECES_IN = {1: 3, PAIRS - 2: 4, PAIRS - 1: 3}


def pieces_of(s):
    if not isinstance(s.n, int) or s.phase + 1 == PHASES or s.g not in PIECES_IN:
        return []
    first = sum(count for g, count in PIECES_IN.items() if g < s.g)
    return [(s.phase + 1, first + i) for i in range(PIECES_IN[s.g])]


def walk(eng, body):
    for phase in range(PHASES):
        first, last = phase * PAIRS // 2, (phase + 1) * PAIRS // 2 - 1
        body(Step(phase, first, 0))
        body(Step(phase, first, 1))
        with eng.Fori(first + 1, last) as half:
            body(Step(phase, half, 0))
            body(Step(phase, half, 1))
        body(Step(phase, last, 0))
        body(Step(phase, last, 1))


def adj_gnn_program(nc, x, adj, weights, vectors, identity, triangles, out):
    x_pairs = x.rearrange("(g k p) d -> g p k d", k=2, p=P)
    out_pairs = out.rearrange("(g k p) d -> g p k d", k=2, p=P)

    ctx = ExitStack()
    with ctx:
        def sb(name, shape, dt=F32):
            return ctx.enter_context(nc.sbuf_tensor(name, shape, dt))

        def bank(name):
            return ctx.enter_context(nc.psum_tensor(name, [P, 512], F32))

        def sem(name):
            return ctx.enter_context(nc.semaphore(name))

        rows = sb("rows", [P, TILES, D])
        weight = sb("weight", [P, 2, 3, CH, 2, D], F32R)
        piece = sb("piece", [P, 2, D])
        vector_rows = sb("vector_rows", [P, 4, D])
        self_bias = sb("self_bias", [P, 2, D], F32R)
        one_64th = sb("one_64th", [P, P], F32R)
        ident = sb("ident", [P, P])
        tri = sb("tri", [P, 3, NODES])
        source = sb("source", [P, 2, D])
        node_t = sb("node_t", [P, 2, 2, CH, 2, P], F32R)
        side_rows = sb("side_rows", [P, 2, D])
        side_parts = sb("side_parts", [P, 2, 2, D], F32R)
        score = sb("score", [P, 2, NODES])
        prob = sb("prob", [P, 2, NODES])
        edge = sb("edge", [P, 2, NODES])
        edge3 = sb("edge3", [P, 2, 3, NODES])
        edge_block = sb("edge_block", [P, 2, 2, P])
        attn_t = sb("attn_t", [P, 2, 2, 2, P], F32R)
        adj_in = sb("adj_in", [P, 2, 2, NODES])
        context = sb("context", [P, 2, D])
        io = sb("io", [P, 2, 2, D])
        row_max = sb("row_max", [P, 2])
        total = sb("total", [P, 2, 2])
        kept = sb("kept", [P, 2])
        diag = sb("diag", [P, 2, 2])
        den = sb("den", [P, 2])
        den_sq = sb("den_sq", [P, 2, 2])
        stats = sb("stats", [P, 2, 6])
        moments = sb("moments", [P, 2, 2])
        spread = sb("spread", [P, 2])
        rstd = sb("rstd", [P, 2])
        in_stats = sb("in_stats", [P, 2, 6])
        in_moments = sb("in_moments", [P, 2, 2])
        in_spread = sb("in_spread", [P, 2])
        in_rstd = sb("in_rstd", [P, 2])
        in_shift = sb("in_shift", [P, 2])
        scalars = sb("scalars", [P, 5])
        minus_half, ln_eps, gate = scalars[:, 0:2], scalars[:, 2:4], scalars[:, 4:5]

        first_raw = rows[:, TILES - PIECES:TILES]

        side_bank = [bank("left_bank"), bank("right_bank")]
        self_bank = bank("self_bank")
        context_bank = bank("context_bank")
        node_bank = bank("node_bank")
        score_bank = bank("score_bank")
        edge_bank = bank("edge_bank")
        scores4 = score_bank[:, :].rearrange("p (k a j) -> p k a j", k=2, a=2)
        node_3 = node_bank[:, 0:D].rearrange("p (c r) -> p c r", c=CH)

        constants_in = sem("constants_in")
        piece_in = [sem("piece_in0"), sem("piece_in1")]
        side_rows_in = sem("side_rows_in")
        norm_rows_in = sem("norm_rows_in")
        x_in = [sem("x_in0"), sem("x_in1")]
        residual_in = [sem("residual_in0"), sem("residual_in1")]
        adj_arrived = sem("adj_arrived")
        out_written = [sem("out_written0"), sem("out_written1")]
        consts_set = sem("consts_set")
        first_in = [sem("first_left_in"), sem("first_right_in"), sem("first_self_in")]
        first_hi = sem("first_hi")
        first_lo = sem("first_lo")
        piece_hi = sem("piece_hi")
        piece_lo = sem("piece_lo")
        bias_lo = sem("bias_lo")
        in_stats_done = sem("in_stats_done")
        in_stats_raw = sem("in_stats_raw")
        in_spread_done = sem("in_spread_done")
        in_rstd_done = sem("in_rstd_done")
        in_shift_done = sem("in_shift_done")
        source_ready = sem("source_ready")
        node_moved = sem("node_moved")
        node_hi = sem("node_hi")
        node_lo = sem("node_lo")
        scored = sem("scored")
        cross_copied = sem("cross_copied")
        score_summed = sem("score_summed")
        max_done = sem("max_done")
        shift_done = sem("shift_done")
        exp_done = sem("exp_done")
        masked_done = sem("masked_done")
        edge_done = sem("edge_done")
        edge3_done = sem("edge3_done")
        kept_done = sem("kept_done")
        diag_done = sem("diag_done")
        den_done = sem("den_done")
        den_sq_done = sem("den_sq_done")
        blocks_placed = sem("blocks_placed")
        edges_moved = sem("edges_moved")
        attn_hi = sem("attn_hi")
        attn_lo = sem("attn_lo")
        side_product = [sem("left_product"), sem("right_product")]
        side_biased = [sem("left_biased"), sem("right_biased")]
        side_hi = [sem("left_hi"), sem("right_hi")]
        side_lo = [sem("left_lo"), sem("right_lo")]
        self_product = sem("self_product")
        self_scaled = sem("self_scaled")
        context_product = sem("context_product")
        context_done = sem("context_done")
        stats_done = sem("stats_done")
        moments_done = sem("moments_done")
        spread_done = sem("spread_done")
        rstd_done = sem("rstd_done")
        centred = sem("centred")
        normed = sem("normed")
        post_done = sem("post_done")

        def piece_part(phase, i, part, where=slice(0, P)):
            if i == 3 * CH:
                return self_bias[where, phase % 2]
            return weight[where, phase % 2, i // CH, i % CH, part]

        block = ctx.enter_context(nc.Block())

        @block.sync
        def _(sp):
            def load_x(s):
                at_least(sp, in_stats_done, 2 * s.n - 2)
                sp.dma_start(rows[:, bass.ds(2 * s.g, 2), :],
                             x_pairs[bass.ds(s.g, 1)].rearrange("g p k d -> p (g k) d")).then_inc(x_in[s.parity], 16)

            def load_residual(s):
                at_least(sp, post_done, s.tile(0) - 2)
                sp.dma_start(io[:, s.parity], x_pairs[bass.ds(s.g, 1)].rearrange("g p k d -> p (g k) d"))\
                  .then_inc(residual_in[s.parity], 16)

            def load_adj(s):
                if s.ahead(-1).bounded:
                    at_least(sp, masked_done, s.before_bounded())
                else:
                    sp.wait_ge(edge_done, s.n)
                sp.dma_start(adj_in[:, :, :, :], adj[:, bass.ds(2 * s.g, 2), :, :]).then_inc(adj_arrived, 16)

            def load_piece(phase, i):
                n = (phase - 1) * PIECES + i
                if i == 1:
                    at_least(sp, bias_lo, phase - 1)
                else:
                    at_least(sp, piece_lo, (phase - 1) * 3 * CH + max(0, i - 1))
                src = weights[phase, i] if i < 3 * CH else vectors[phase, ROW_SELF].partition_broadcast(P)
                sp.dma_start(piece[:, n % 2], src).then_inc(piece_in[n % 2], 16)

            def load_side_rows(phase):
                for side in (LEFT, RIGHT):
                    at_least(sp, side_biased[side], 2 * PAIRS * phase)
                    sp.dma_start(vector_rows[:, ROW_LEFT + side], vectors[phase, ROW_LEFT + side].partition_broadcast(P))\
                      .then_inc(side_rows_in, 16)

            def load_norm_rows(phase):
                at_least(sp, post_done, 2 * PAIRS * phase)
                for v in (ROW_GAMMA, ROW_BETA):
                    sp.dma_start(vector_rows[:, v], vectors[phase, v].partition_broadcast(P)).then_inc(norm_rows_in, 16)

            def store(s):
                at_least(sp, post_done, s.tile(2))
                sp.dma_start(out_pairs[bass.ds(s.g, 1)].rearrange("g p k d -> p (g k) d"), io[:, s.parity])\
                  .then_inc(out_written[s.parity], 16)

            def body(s):
                prev, nxt, after = s.ahead(-1), s.ahead(1), s.ahead(2)
                if isinstance(s.n, int) and s.g == 0 and s.phase > 0:
                    load_side_rows(s.phase)
                if after.exists() and after.phase == 0:
                    load_x(after)
                if nxt.exists():
                    load_adj(nxt)
                if nxt.exists() and nxt.phase == 1:
                    load_residual(nxt)
                if isinstance(s.n, int) and s.g == 0 and s.phase > 0:
                    load_norm_rows(s.phase)
                if prev.exists() and prev.phase == 2:
                    store(prev)
                for phase, i in pieces_of(s):
                    load_piece(phase, i)

            def load_first(w):
                sp.dma_start(first_raw[:, w * CH:(w + 1) * CH], weights[0, w * CH:(w + 1) * CH].rearrange("c p e -> p c e"))\
                  .then_inc(first_in[w], 16)

            load_x(Step(0, 0, 0))
            sp.dma_start(ident[:, :], identity).then_inc(constants_in, 16)
            load_first(LEFT)
            load_adj(Step(0, 0, 0))
            sp.dma_start(tri[:, :, :], triangles).then_inc(constants_in, 16)
            load_first(RIGHT)
            load_x(Step(0, 0, 1))
            load_side_rows(0)
            sp.dma_start(first_raw[:, 3 * CH], vectors[0, ROW_SELF].partition_broadcast(P)).then_inc(first_in[SELF], 16)
            load_first(SELF)
            load_norm_rows(0)
            walk(sp, body)
            store(Step(2, STEPS // 2 - 1, 1))
            for parity in range(2):
                sp.wait_ge(out_written[parity], 16 * PAIRS // 2)

        @block.tensor
        def _(pe):
            def transpose_nodes(s, k):
                pe.wait_ge(source_ready, s.tile(k) + 1)
                at_least(pe, node_lo, s.tile(k))
                for c in range(CH):
                    mm = nc.tensor.transpose(node_bank[:, c * P:(c + 1) * P], source[:, k, c * P:(c + 1) * P], ident[:, :])
                mm.then_inc(node_moved, 1)

            def scores(s):
                pe.wait_ge(node_hi, s.tile(2))
                pe.wait_ge(node_lo, s.tile(2))
                at_least(pe, score_summed, 2 * s.n)
                for k in range(2):
                    for c in range(CH):
                        t = node_t[:, s.parity, k, c].rearrange("p a r -> p (a r)")
                        nc.tensor.matmul(score_bank[:, k * 256:(k + 1) * 256], t[:, 0:P], t,
                                         start=(c == 0), stop=False, skip_group_check=True)
                        mm = nc.tensor.matmul(score_bank[:, k * 256:k * 256 + P], t[:, P:2 * P], t[:, 0:P],
                                              start=False, stop=(c == CH - 1), skip_group_check=True)
                mm.then_inc(scored, 1)

            def transpose_edges(s):
                pe.wait_ge(blocks_placed, 2 * s.n + 2)
                pe.wait_ge(attn_lo, s.n)
                for k in range(2):
                    for ul in range(2):
                        at = (2 * k + ul) * P
                        mm = nc.tensor.transpose(edge_bank[:, at:at + P], edge_block[:, k, ul], ident[:, :])
                mm.then_inc(edges_moved, 1)

            def project(s, k, w, bank, done):
                for c in range(CH):
                    for a, b in ((HI, HI), (HI, LO), (LO, HI)):
                        last = w != SELF and (c, a) == (CH - 1, LO)
                        mm = nc.tensor.matmul(bank[:, 0:D], node_t[:, s.parity, k, c, a], weight[:, s.phase % 2, w, c, b],
                                              start=(c == 0 and a == b), stop=last)
                if w == SELF:
                    mm = nc.tensor.matmul(bank[:, 0:D], one_64th[:, :], self_bias[:, s.phase % 2], start=False, stop=True)
                mm.then_inc(done, 1)

            def project_side(s, k, side):
                if side == LEFT:
                    pe.wait_ge(node_hi, s.tile(k) + 1)
                    pe.wait_ge(node_lo, s.tile(k) + 1)
                at_least(pe, side_biased[side], s.tile(k))
                if is_first(s) and k == 0:
                    pe.wait_ge(first_lo, CH * (side + 1))
                project(s, k, side, side_bank[side], side_product[side])

            def project_self(s, k):
                at_least(pe, self_scaled, s.tile(k))
                if is_first(s) and k == 0:
                    pe.wait_ge(first_lo, PIECES)
                project(s, k, SELF, self_bank, self_product)

            def weigh(s, k):
                pe.wait_ge(attn_hi, s.n + 1)
                pe.wait_ge(attn_lo, s.n + 1)
                at_least(pe, context_done, s.tile(k))
                for side in (LEFT, RIGHT):
                    triangle = 1 - side if s.bounded else side
                    pe.wait_ge(side_hi[side], s.tile(k) + 1)
                    pe.wait_ge(side_lo[side], s.tile(k) + 1)
                    for a, b in ((HI, HI), (HI, LO), (LO, HI)):
                        mm = nc.tensor.matmul(context_bank[:, 0:D], attn_t[:, a, k, triangle], side_parts[:, side, b],
                                              start=(side == LEFT and a == b), stop=(side == RIGHT and a == LO))
                mm.then_inc(context_product, 1)

            def body(s):
                prev, nxt = s.ahead(-1), s.ahead(1)
                if isinstance(s.n, int) and s.g == 0 and s.phase > 0:
                    pe.wait_ge(piece_lo, s.phase * 3 * CH)
                    pe.wait_ge(bias_lo, s.phase)
                project_side(s, 0, LEFT)
                if prev.exists():
                    weigh(prev, 1)
                if nxt.exists():
                    transpose_nodes(nxt, 0)
                project_side(s, 0, RIGHT)
                if not s.bounded:
                    transpose_edges(s)
                if nxt.exists():
                    transpose_nodes(nxt, 1)
                project_self(s, 0)
                project_side(s, 1, LEFT)
                weigh(s, 0)
                if nxt.exists():
                    scores(nxt)
                project_side(s, 1, RIGHT)
                project_self(s, 1)

            pe.wait_ge(constants_in, 32)
            pe.wait_ge(consts_set, 1)
            start = Step(0, 0, 0)
            transpose_nodes(start, 0)
            transpose_nodes(start, 1)
            scores(start)
            walk(pe, body)
            weigh(Step(2, STEPS // 2 - 1, 1), 1)

        @block.scalar
        def _(act):
            def fill_source(s, k):
                at_least(act, node_moved, s.tile(k) - 1)
                if s.phase == 1:
                    nc.scalar.activation(source[:, k:k + 1], rows[:, s.slot(k)], ACT.Copy).then_inc(source_ready, 1)
                else:
                    act.wait_ge(in_shift_done, s.normal + 1)
                    nc.scalar.activation(source[:, k:k + 1], rows[:, s.slot(k)], ACT.Identity, bias=in_shift[:, k:k + 1],
                                         scale=in_rstd[:, k:k + 1]).then_inc(source_ready, 1)

            def split_nodes(s, k):
                act.wait_ge(node_moved, s.tile(k) + 1)
                nc.scalar.activation(node_t[:, s.parity, k, :, HI], node_3, ACT.Relu).then_inc(node_hi, 1)

            def copy_cross(s):
                act.wait_ge(scored, s.n + 1)
                at_least(act, kept_done, s.n)
                for h, half in enumerate(HALVES):
                    nc.scalar.activation(score[half], scores4[half, :, 1, h * NODES:(h + 1) * NODES], ACT.Copy)\
                      .then_inc(cross_copied, 1)

            def exponentials(s):
                if s.bounded:
                    act.wait_ge(score_summed, 2 * s.n + 2)
                else:
                    act.wait_ge(shift_done, s.n + 1 - PAIRS)
                at_least(act, masked_done, s.before_bounded())
                at_least(act, edge_done, s.n)
                for k in range(2):
                    nc.scalar.activation(prob[:, k], score[:, k], ACT.Exp, scale=SCALE,
                                         accum_out=total[:, s.parity, k:k + 1]).then_inc(exp_done, 1)

            def place_blocks(s):
                act.wait_ge(edge3_done, s.n + 1)
                if s.ahead(-1).bounded:
                    at_least(act, attn_lo, s.n)
                else:
                    act.wait_ge(edges_moved, s.n - PAIRS)
                for h, half in enumerate(HALVES):
                    nc.scalar.activation(edge_block[half, :, :, h * NODES:(h + 1) * NODES], edge3[half, :, 0:2], ACT.Copy)\
                      .then_inc(blocks_placed, 1)

            def split_edges(s):
                if s.bounded:
                    act.wait_ge(blocks_placed, 2 * s.n + 2)
                    at_least(act, context_product, s.tile(0))
                    blocks = edge_block[:, :, :, :].rearrange("p k u r -> p (k u r)")
                else:
                    act.wait_ge(edges_moved, s.n + 1 - PAIRS)
                    blocks = edge_bank[:, :]
                nc.scalar.activation(attn_t[:, HI].rearrange("p k u r -> p (k u r)"), blocks, ACT.Copy).then_inc(attn_hi, 1)

            def split_side(s, k, side):
                act.wait_ge(side_biased[side], s.tile(k) + 1)
                at_least(act, context_product, s.tile(k))
                nc.scalar.activation(side_parts[:, side, HI], side_rows[:, side], ACT.Copy).then_inc(side_hi[side], 1)

            def scale_self(s, k):
                act.wait_ge(self_product, s.tile(k) + 1)
                act.wait_ge(diag_done, s.n + 1)
                at_least(act, post_done, s.tile(k) - 1)
                nc.scalar.activation(context[:, k], self_bank[:, 0:D], ACT.Identity,
                                     scale=diag[:, s.parity, k:k + 1]).then_inc(self_scaled, 1)

            def split_piece(phase, i):
                n = (phase - 1) * PIECES + i
                act.wait_ge(piece_in[n % 2], 16 * (n // 2 + 1))
                nc.scalar.activation(piece_part(phase, i, HI), piece[:, n % 2], ACT.Copy).then_inc(piece_hi, 1)

            def split_first(i):
                if i % CH == 0:
                    act.wait_ge(first_in[min(i // CH, SELF)], 32 if i // CH == SELF else 16)
                nc.scalar.activation(piece_part(0, i, HI), first_raw[:, i], ACT.Copy).then_inc(first_hi, 1)

            def body(s):
                prev, nxt, after = s.ahead(-1), s.ahead(1), s.ahead(2)
                pieces = pieces_of(s)
                if prev.exists():
                    scale_self(prev, 1)
                if not s.bounded:
                    place_blocks(s)
                split_side(s, 0, LEFT)
                if nxt.exists():
                    split_nodes(nxt, 0)
                if s.bounded:
                    place_blocks(s)
                split_edges(s)
                split_side(s, 0, RIGHT)
                if nxt.exists():
                    split_nodes(nxt, 1)
                if len(pieces) > 0:
                    split_piece(*pieces[0])
                scale_self(s, 0)
                split_side(s, 1, LEFT)
                if len(pieces) > 1:
                    split_piece(*pieces[1])
                if nxt.exists():
                    copy_cross(nxt)
                    if not nxt.bounded:
                        exponentials(nxt)
                if len(pieces) > 2:
                    split_piece(*pieces[2])
                split_side(s, 1, RIGHT)
                if len(pieces) > 3:
                    split_piece(*pieces[3])
                if after.exists():
                    fill_source(after, 0)
                if nxt.exists() and nxt.bounded:
                    exponentials(nxt)
                if after.exists():
                    fill_source(after, 1)

            start = Step(0, 0, 0)
            fill_source(start, 0)
            fill_source(start, 1)
            act.wait_ge(consts_set, 1)
            split_nodes(start, 0)
            split_nodes(start, 1)
            for i in range(CH):
                split_first(i)
            copy_cross(start)
            exponentials(start)
            for i in range(CH, PIECES):
                split_first(i)
            fill_source(start.ahead(1), 0)
            fill_source(start.ahead(1), 1)
            walk(act, body)
            scale_self(Step(2, STEPS // 2 - 1, 1), 1)

        @block.vector
        def _(dve):
            def input_stats(s, k):
                if s.phase == 0:
                    dve.wait_ge(x_in[s.parity], 16 * (s.half + 1))
                at_least(dve, in_rstd_done, s.normal)
                nc.vector.bn_stats(in_stats[:, k], rows[:, s.slot(k)]).then_inc(in_stats_raw, 1)

            def gather_input(s, k):
                dve.wait_ge(in_stats_raw, 2 * s.normal + k + 1)
                nc.vector.memset(gate[:, :], 0.0)
                nc.vector.bn_aggr(in_moments[:, k], in_stats[:, k]).then_inc(in_stats_done, 1)

            def input_shift(s):
                dve.wait_ge(in_rstd_done, s.normal + 1)
                at_least(dve, source_ready, s.tile(0))
                nc.vector.scalar_tensor_tensor(in_shift[:, :], in_moments[:, :, 0], -1.0, in_rstd[:, :],
                                               ALU.mult, ALU.mult).then_inc(in_shift_done, 1)

            def split_nodes(s, k):
                dve.wait_ge(node_hi, s.tile(k) + 1)
                nc.vector.scalar_tensor_tensor(node_t[:, s.parity, k, :, LO], node_3, 0.0,
                                               node_t[:, s.parity, k, :, HI].bitcast(F32),
                                               ALU.max, ALU.subtract).then_inc(node_lo, 1)

            def sum_scores(s):
                dve.wait_ge(cross_copied, 2 * s.n + 2)
                for h, half in enumerate(HALVES):
                    nc.vector.tensor_tensor(score[half], scores4[half, :, 0, h * NODES:(h + 1) * NODES], score[half],
                                            ALU.add).then_inc(score_summed, 1)

            def shift_scores(s):
                dve.wait_ge(score_summed, 2 * s.n + 2)
                nc.vector.tensor_reduce(row_max[:, :], score[:, :, :], op=ALU.max, axis=AX.X).then_inc(max_done, 1)
                dve.wait_ge(max_done, s.n + 1 - PAIRS)
                nc.vector.tensor_tensor(score[:, :, :], score[:, :, :],
                                        row_max[:, :].unsqueeze(2).to_broadcast([P, 2, NODES]),
                                        ALU.subtract).then_inc(shift_done, 1)

            def edges(s):
                dve.wait_ge(exp_done, 2 * s.n + 2)
                dve.wait_ge(adj_arrived, 16 * (s.n + 1))
                at_least(dve, edge3_done, s.n)
                nc.vector.tensor_tensor(edge[:, :, :], prob[:, :, :], adj_in[:, :, int(s.bounded)], ALU.mult).then_inc(edge_done, 1)
                if s.bounded:
                    nc.vector.tensor_tensor(score[:, :, :], prob[:, :, :], adj_in[:, :, 0], ALU.mult).then_inc(masked_done, 1)
                    dve.wait_ge(masked_done, s.before_bounded() + 1)
                    masked = score
                else:
                    dve.wait_ge(edge_done, s.n + 1)
                    masked = edge
                nc.vector.tensor_reduce(kept[:, :], masked[:, :, :], op=ALU.add, axis=AX.X).then_inc(kept_done, 1)

            def denominator(s):
                dve.wait_ge(kept_done, s.n + 1)
                nc.vector.scalar_tensor_tensor(den[:, :], total[:, s.parity], GUARD, kept[:, :],
                                               ALU.mult, ALU.add).then_inc(den_done, 1)

            def diagonal(s):
                dve.wait_ge(edge3_done, s.n + 1)
                nc.vector.tensor_reduce(diag[:, s.parity], edge3[:, :, 2], op=ALU.add, axis=AX.X).then_inc(diag_done, 1)

            def squared_denominator(s):
                dve.wait_ge(den_done, s.n + 1)
                nc.vector.tensor_tensor(den_sq[:, s.parity], den[:, :], den[:, :], ALU.mult).then_inc(den_sq_done, 1)

            def split_first(i):
                dve.wait_ge(first_hi, i + 1)
                low = slice(0, P) if i < 3 * CH else HALVES[1]
                nc.vector.tensor_tensor(piece_part(0, i, LO, low), first_raw[low, i], piece_part(0, i, HI, low).bitcast(F32),
                                        ALU.subtract).then_inc(first_lo, 1)

            def split_self_bias(phase):
                n = phase * PIECES - 1
                low = HALVES[1]
                dve.wait_ge(piece_hi, n + 1)
                nc.vector.tensor_tensor(self_bias[low, phase % 2], piece[low, n % 2], self_bias[low, phase % 2].bitcast(F32),
                                        ALU.subtract).then_inc(bias_lo, 1)

            def split_edges(s):
                dve.wait_ge(attn_hi, s.n + 1)
                blocks = edge_block[:, :, :, :].rearrange("p k u r -> p (k u r)") if s.bounded else edge_bank[:, :]
                nc.vector.tensor_tensor(attn_t[:, LO].rearrange("p k u r -> p (k u r)"), blocks,
                                        attn_t[:, HI].rearrange("p k u r -> p (k u r)").bitcast(F32),
                                        ALU.subtract).then_inc(attn_lo, 1)

            def add_bias(s, k, side):
                dve.wait_ge(side_product[side], s.tile(k) + 1)
                at_least(dve, side_lo[side], s.tile(k))
                if isinstance(s.n, int) and s.g == 0:
                    dve.wait_ge(side_rows_in, 32 * (s.phase + 1))
                nc.vector.tensor_tensor(side_rows[:, side], side_bank[side][:, 0:D], vector_rows[:, ROW_LEFT + side],
                                        ALU.add).then_inc(side_biased[side], 1)

            def sum_context(s, k):
                dve.wait_ge(context_product, s.tile(k) + 1)
                dve.wait_ge(self_scaled, s.tile(k) + 1)
                nc.vector.tensor_tensor(context[:, k], context_bank[:, 0:D], context[:, k], ALU.add).then_inc(context_done, 1)

            def context_stats(s, k):
                dve.wait_ge(context_done, s.tile(k) + 1)
                nc.vector.bn_stats(stats[:, k], context[:, k]).then_inc(stats_done, 1)

            def gather_moments(s, k):
                dve.wait_ge(stats_done, s.tile(k) + 1)
                nc.vector.memset(gate[:, :], 0.0)
                nc.vector.bn_aggr(moments[:, k], stats[:, k]).then_inc(moments_done, 1)

            def spreads(s):
                dve.wait_ge(moments_done, s.tile(2))
                dve.wait_ge(den_sq_done, s.n + 1)
                nc.vector.scalar_tensor_tensor(spread[:, :], den_sq[:, s.parity], GNN_EPS, moments[:, :, 1],
                                               ALU.mult, ALU.add).then_inc(spread_done, 1)

            def centre(s, k):
                if isinstance(s.n, int) and s.g == 0:
                    dve.wait_ge(norm_rows_in, 32 * (s.phase + 1))
                dve.wait_ge(moments_done, s.tile(k) + 1)
                nc.vector.scalar_tensor_tensor(context[:, k], context[:, k], moments[:, k, 0:1], vector_rows[:, ROW_GAMMA],
                                               ALU.subtract, ALU.mult).then_inc(centred, 1)

            def norm(s, k):
                dve.wait_ge(rstd_done, s.n + 1)
                dve.wait_ge(centred, s.tile(k) + 1)
                to, done = (rows[:, s.slot(k)], post_done) if s.phase == 0 else (context[:, k:k + 1], normed)
                nc.vector.scalar_tensor_tensor(to, context[:, k:k + 1], rstd[:, k:k + 1], vector_rows[:, ROW_BETA:ROW_BETA + 1],
                                               ALU.mult, ALU.add).then_inc(done, 1)

            def residual(s, k):
                dve.wait_ge(normed, s.tile(k) + 1 - 2 * PAIRS)
                if s.phase == 1:
                    dve.wait_ge(residual_in[s.parity], 16 * (s.half + 1 - PAIRS // 2))
                    other, to = io[:, s.parity, k:k + 1], rows[:, s.slot(k)]
                else:
                    at_least(dve, out_written[s.parity], 16 * (s.half - PAIRS))
                    other, to = rows[:, s.slot(k)], io[:, s.parity, k:k + 1]
                nc.vector.scalar_tensor_tensor(to, context[:, k:k + 1], 0.0, other, ALU.max, ALU.add).then_inc(post_done, 1)

            def body(s):
                prev, nxt, after = s.ahead(-1), s.ahead(1), s.ahead(2)
                normal = after.exists() and after.bounded
                add_bias(s, 0, LEFT)
                denominator(s)
                if prev.exists():
                    sum_context(prev, 1)
                diagonal(s)
                if prev.exists():
                    context_stats(prev, 1)
                squared_denominator(s)
                if nxt.exists():
                    split_nodes(nxt, 0)
                if prev.exists():
                    gather_moments(prev, 1)
                    centre(prev, 0)
                    spreads(prev)
                    centre(prev, 1)
                add_bias(s, 0, RIGHT)
                split_edges(s)
                if prev.exists():
                    norm(prev, 0)
                if nxt.exists():
                    split_nodes(nxt, 1)
                if prev.exists():
                    norm(prev, 1)
                    if prev.phase > 0:
                        residual(prev, 0)
                if normal:
                    input_stats(after, 0)
                if prev.exists() and prev.phase > 0:
                    residual(prev, 1)
                if normal:
                    gather_input(after, 0)
                add_bias(s, 1, LEFT)
                if normal:
                    input_stats(after, 1)
                sum_context(s, 0)
                if normal:
                    gather_input(after, 1)
                context_stats(s, 0)
                if nxt.exists() and nxt.bounded:
                    add_bias(s, 1, RIGHT)
                if nxt.exists():
                    sum_scores(nxt)
                gather_moments(s, 0)
                if nxt.exists() and not nxt.bounded:
                    shift_scores(nxt)
                if not (nxt.exists() and nxt.bounded):
                    add_bias(s, 1, RIGHT)
                for phase, i in pieces_of(s):
                    if i == 3 * CH:
                        split_self_bias(phase)
                if normal:
                    input_shift(after)
                if nxt.exists():
                    edges(nxt)

            start = Step(0, 0, 0)
            nc.vector.memset(edge_block[:, :, :, :], 0.0)
            nc.vector.memset(minus_half[:, :], -0.5)
            nc.vector.memset(ln_eps[:, :], LN_EPS)
            nc.vector.memset(one_64th[:, :].bitcast(F32), 1.0 / 64).then_inc(consts_set, 1)
            for k in range(2):
                input_stats(start, k)
                gather_input(start, k)
            input_shift(start)
            split_nodes(start, 0)
            split_nodes(start, 1)
            for i in range(CH):
                split_first(i)
            sum_scores(start)
            edges(start)
            for i in range(CH, PIECES):
                split_first(i)
            for k in range(2):
                input_stats(start.ahead(1), k)
                gather_input(start.ahead(1), k)
            input_shift(start.ahead(1))
            walk(dve, body)
            final = Step(2, STEPS // 2 - 1, 1)
            sum_context(final, 1)
            context_stats(final, 1)
            gather_moments(final, 1)
            spreads(final)
            for k in range(2):
                centre(final, k)
                norm(final, k)
                residual(final, k)

        @block.gpsimd
        def _(pool):
            def input_rstd(s):
                pool.wait_ge(in_stats_done, 2 * s.normal + 2)
                at_least(pool, source_ready, s.tile(0))
                nc.gpsimd.tensor_tensor(in_spread[:, :], in_moments[:, :, 1], ln_eps[:, :], ALU.add).then_inc(in_spread_done, 1)
                pool.wait_ge(in_spread_done, s.normal + 1)
                nc.gpsimd.tensor_tensor(in_rstd[:, :], in_spread[:, :], minus_half[:, :], ALU.pow).then_inc(in_rstd_done, 1)

            def output_rstd(s):
                pool.wait_ge(spread_done, s.n + 1)
                nc.gpsimd.tensor_tensor(rstd[:, :], spread[:, :], minus_half[:, :], ALU.pow).then_inc(rstd_done, 1)

            def split_side(s, k, side):
                pool.wait_ge(side_hi[side], s.tile(k) + 1)
                nc.gpsimd.tensor_tensor(side_parts[:, side, LO], side_rows[:, side], side_parts[:, side, HI].bitcast(F32),
                                        ALU.subtract).then_inc(side_lo[side], 1)

            def triangles_of(s):
                pool.wait_ge(edge_done, s.n + 1)
                at_least(pool, blocks_placed, 2 * s.n)
                at_least(pool, diag_done, s.n)
                nc.gpsimd.tensor_tensor(edge3[:, :, :, :], edge[:, :, :].unsqueeze(2).to_broadcast([P, 2, 3, NODES]),
                                        tri[:, :, :].unsqueeze(1).to_broadcast([P, 2, 3, NODES]), ALU.mult).then_inc(edge3_done, 1)

            def split_piece(phase, i):
                if i < 3 * CH:
                    n = (phase - 1) * PIECES + i
                    pool.wait_ge(piece_hi, n + 1)
                    nc.gpsimd.tensor_tensor(piece_part(phase, i, LO), piece[:, n % 2], piece_part(phase, i, HI).bitcast(F32),
                                            ALU.subtract).then_inc(piece_lo, 1)

            def body(s):
                prev, nxt, after = s.ahead(-1), s.ahead(1), s.ahead(2)
                pieces = pieces_of(s)
                split_side(s, 0, LEFT)
                if prev.exists():
                    output_rstd(prev)
                split_side(s, 0, RIGHT)
                if len(pieces) > 0:
                    split_piece(*pieces[0])
                split_side(s, 1, LEFT)
                if len(pieces) > 1:
                    split_piece(*pieces[1])
                if after.exists() and after.phase != 1:
                    input_rstd(after)
                if len(pieces) > 2:
                    split_piece(*pieces[2])
                split_side(s, 1, RIGHT)
                if nxt.exists():
                    triangles_of(nxt)
                if len(pieces) > 3:
                    split_piece(*pieces[3])

            pool.wait_ge(constants_in, 32)
            pool.wait_ge(consts_set, 1)
            start = Step(0, 0, 0)
            input_rstd(start)
            triangles_of(start)
            input_rstd(start.ahead(1))
            walk(pool, body)
            output_rstd(Step(2, STEPS // 2 - 1, 1))


def kernel(**inputs):
    import numpy as np
    import concourse.bacc as bacc
    from concourse.bass_utils import run_bass_kernel_spmd

    given = {name: np.asarray(value) for name, value in inputs.items()}

    def layer(kind, name):
        return [given["L0_gnn_" + kind[0]][0], given["L0_gnn_" + kind[0]][1], given["L1_gnn_" + kind[1]]][name]

    matrices = [[layer(kind, n) for kind in (("Wl", "W_left"), ("Wr", "W_right"), ("Ws", "W_self"))] for n in range(PHASES)]
    rows = [[layer(kind, n) for kind in (("ln_w", "gamma"), ("ln_b", "beta"), ("bl", "b_left"), ("br", "b_right"), ("bs", "b_self"))]
            for n in range(PHASES)]
    below = np.tril(np.ones((NODES, NODES), np.float32), -1)
    triangles = np.stack([below.T, below, np.eye(NODES, dtype=np.float32)], axis=1)
    arrays = {
        "x": np.ascontiguousarray(given["x"].reshape(TILES * P, D)),
        "adj": np.ascontiguousarray(np.stack([given["adj"], given["adj"].transpose(0, 2, 1)], axis=2)
                                    .reshape(TILES, P, 2, NODES).transpose(1, 0, 2, 3)),
        "weights": np.ascontiguousarray(np.stack([np.stack([m.T.reshape(CH, P, D) for m in ms]) for ms in matrices])
                                        .reshape(PHASES, 3 * CH, P, D)),
        "vectors": np.ascontiguousarray(np.stack([np.stack(r) for r in rows])),
        "identity": np.eye(P, dtype=np.float32),
        "triangles": np.concatenate([triangles, triangles]),
    }
    nc = bacc.Bacc("TRN2", target_bir_lowering=False, num_devices=1)
    aps = [nc.dram_tensor(name, a.shape, mybir.dt.from_np(a.dtype), kind="ExternalInput").ap() for name, a in arrays.items()]
    out = nc.dram_tensor("out", (TILES * P, D), F32, kind="ExternalOutput").ap()
    adj_gnn_program(nc, *aps, out)
    result = run_bass_kernel_spmd(nc, [arrays], core_ids=[0])
    return result.results[0]["out"].reshape(TILES * P // NODES, NODES, D)
```

```python
import concourse.bass as bass
from concourse import mybir
from contextlib import ExitStack

F32 = mybir.dt.float32
F32R = mybir.dt.float32r
ALU = mybir.AluOpType
ACT = mybir.ActivationFunctionType
AX = mybir.AxisListType

P = 128
NODES = 64
D = 384
CH = D // P
TILES = 64
PAIRS = TILES // 2
PHASES = 3
STEPS = PHASES * PAIRS
SCALE = float(D) ** -0.5
LN_EPS = 1e-5
GNN_EPS = 1e-12
GUARD = 1e-10
WARM_UP = 3
HI, LO = 0, 1
LEFT, RIGHT, SELF = 0, 1, 2
ROW_GAMMA, ROW_BETA, ROW_LEFT, ROW_RIGHT, ROW_SELF = range(5)
PIECES = 3 * CH
HALVES = (slice(0, NODES), slice(NODES, P))


class Step:

    def __init__(self, phase, half, parity):
        self.half, self.parity = half, parity
        self.n = 2 * half + parity
        self.phase = self.n // PAIRS if isinstance(half, int) else phase
        self.g = self.n - PAIRS * self.phase
        self.bounded = self.phase != 1
        self.normal = self.n - (PAIRS if self.phase == 2 else 0)

    def before_bounded(self):
        return self.normal if self.bounded else PAIRS

    def ahead(self, k):
        parity = self.parity + k
        return Step(self.phase, self.half + parity // 2, parity % 2)

    def exists(self):
        return not isinstance(self.n, int) or 0 <= self.n < STEPS

    def tile(self, k):
        return 2 * self.n + k

    def slot(self, k):
        return bass.ds(2 * self.g + k, 1)


def at_least(eng, sem, value):
    if not isinstance(value, int) or value > 0:
        eng.wait_ge(sem, value)


PIECES_IN = {1: 2, PAIRS - 4: 1, PAIRS - 3: 2, PAIRS - 2: 2, PAIRS - 1: 2}


def pieces_of(s):
    if not isinstance(s.n, int) or s.phase + 1 == PHASES or s.g not in PIECES_IN:
        return []
    first = sum(count for g, count in PIECES_IN.items() if g < s.g)
    return [(s.phase + 1, first + i) for i in range(PIECES_IN[s.g])]


def walk(eng, body):
    for phase in range(PHASES):
        first, last = phase * PAIRS // 2, (phase + 1) * PAIRS // 2 - 1
        body(Step(phase, first, 0))
        body(Step(phase, first, 1))
        with eng.Fori(first + 1, last - 1) as half:
            body(Step(phase, half, 0))
            body(Step(phase, half, 1))
        for half in (last - 1, last):
            body(Step(phase, half, 0))
            body(Step(phase, half, 1))


def adj_gnn_program(nc, x, adj, weights, vectors, identity, triangles, out):
    x_pairs = x.rearrange("(g k p) d -> g p k d", k=2, p=P)
    out_pairs = out.rearrange("(g k p) d -> g p k d", k=2, p=P)

    ctx = ExitStack()
    with ctx:
        def sb(name, shape, dt=F32):
            return ctx.enter_context(nc.sbuf_tensor(name, shape, dt))

        def bank(name):
            return ctx.enter_context(nc.psum_tensor(name, [P, 512], F32))

        def sem(name):
            return ctx.enter_context(nc.semaphore(name))

        rows = sb("rows", [P, TILES, D])
        weight = sb("weight", [P, 2, 3, CH, 2, D], F32R)
        piece = sb("piece", [P, 2, D])
        vector_rows = sb("vector_rows", [P, 5, D])
        ident_r = sb("ident_r", [P, P], F32R)
        tri = sb("tri", [P, 3, NODES])
        source = sb("source", [P, 2, D])
        node_t = sb("node_t", [P, 2, 2, CH, 2, P], F32R)
        side_rows = sb("side_rows", [P, 2, D])
        side_parts = sb("side_parts", [P, 2, 2, D], F32R)
        score = sb("score", [P, 2, NODES])
        edge = sb("edge", [P, 2, NODES])
        cross = sb("cross", [P, 2, P], F32R)
        edge3 = sb("edge3", [P, 2, 3, NODES])
        edge_block = sb("edge_block", [P, 2, 2, P])
        attn_t = sb("attn_t", [P, 2, 2, 2, P], F32R)
        adj_in = sb("adj_in", [P, 2, 2, NODES])
        context = sb("context", [P, 2, D])
        self_rows = sb("self_rows", [P, D])
        io = sb("io", [P, 2, 2, D])
        row_max = sb("row_max", [P, 2])
        total = sb("total", [P, 2, 2])
        kept = sb("kept", [P, 2])
        diag = sb("diag", [P, 2, 2])
        den = sb("den", [P, 2])
        den_sq = sb("den_sq", [P, 2, 2])
        stats = sb("stats", [P, 2, 6])
        moments = sb("moments", [P, 2, 2])
        spread = sb("spread", [P, 2])
        rstd = sb("rstd", [P, 2])
        in_stats = sb("in_stats", [P, 2, 6])
        in_moments = sb("in_moments", [P, 2, 2])
        in_spread = sb("in_spread", [P, 2])
        in_rstd = sb("in_rstd", [P, 2])
        in_shift = sb("in_shift", [P, 2])
        scalars = sb("scalars", [P, 8])
        minus_half, ln_eps, gate = scalars[:, 0:2], scalars[:, 2:4], scalars[:, 4:8]

        ident = ident_r[:, :].bitcast(F32)
        first_raw = rows[:, TILES - PIECES:TILES]

        side_bank = [bank("left_bank"), bank("right_bank")]
        self_bank = bank("self_bank")
        context_bank = bank("context_bank")
        node_bank = [bank("node_bank0"), bank("node_bank1")]
        score_bank = bank("score_bank")
        edge_bank = bank("edge_bank")
        scores4 = score_bank[:, :].rearrange("p (k a j) -> p k a j", k=2, a=2)
        node_3 = [b[:, 0:D].rearrange("p (c r) -> p c r", c=CH) for b in node_bank]

        identity_in = sem("identity_in")
        triangles_in = sem("triangles_in")
        piece_in = [sem("piece_in0"), sem("piece_in1")]
        side_rows_in = sem("side_rows_in")
        self_row_in = sem("self_row_in")
        norm_rows_in = sem("norm_rows_in")
        x_in = [sem("x_in0"), sem("x_in1")]
        residual_in = [sem("residual_in0"), sem("residual_in1")]
        adj_arrived = sem("adj_arrived")
        out_written = [sem("out_written0"), sem("out_written1")]
        consts_set = sem("consts_set")
        ident_rounded = sem("ident_rounded")
        first_in = [sem("first_left_in"), sem("first_right_in"), sem("first_self_in")]
        first_hi = [sem("first_left_hi"), sem("first_right_hi"), sem("first_self_hi")]
        first_lo = [sem("first_left_lo"), sem("first_right_lo"), sem("first_self_lo")]
        piece_hi = sem("piece_hi")
        piece_lo = sem("piece_lo")
        in_stats_done = sem("in_stats_done")
        in_stats_raw = sem("in_stats_raw")
        in_spread_done = sem("in_spread_done")
        in_rstd_done = sem("in_rstd_done")
        in_shift_done = sem("in_shift_done")
        source_ready = sem("source_ready")
        node_moved = sem("node_moved")
        node_hi = sem("node_hi")
        node_lo = sem("node_lo")
        scored = sem("scored")
        cross_copied = sem("cross_copied")
        cross_turned = sem("cross_turned")
        score_summed = sem("score_summed")
        max_done = sem("max_done")
        shift_done = sem("shift_done")
        exp_done = sem("exp_done")
        masked_done = sem("masked_done")
        edge_done = sem("edge_done")
        edge3_done = sem("edge3_done")
        kept_done = sem("kept_done")
        diag_done = sem("diag_done")
        den_done = sem("den_done")
        den_sq_done = sem("den_sq_done")
        blocks_placed = sem("blocks_placed")
        edges_moved = sem("edges_moved")
        attn_hi = sem("attn_hi")
        attn_lo = sem("attn_lo")
        side_product = [sem("left_product"), sem("right_product")]
        side_biased = [sem("left_biased"), sem("right_biased")]
        side_hi = [sem("left_hi"), sem("right_hi")]
        side_lo = [sem("left_lo"), sem("right_lo")]
        self_product = sem("self_product")
        self_scaled = sem("self_scaled")
        self_bias_scaled = sem("self_bias_scaled")
        self_biased = sem("self_biased")
        context_product = sem("context_product")
        context_done = sem("context_done")
        stats_done = sem("stats_done")
        moments_done = sem("moments_done")
        spread_done = sem("spread_done")
        rstd_done = sem("rstd_done")
        centred = sem("centred")
        normed = sem("normed")
        post_done = sem("post_done")

        def piece_part(phase, i, part):
            return weight[:, phase % 2, i // CH, i % CH, part]

        block = ctx.enter_context(nc.Block())

        @block.sync
        def _(sp):
            def load_x(s):
                at_least(sp, in_stats_done, 2 * s.n - 2)
                sp.dma_start(rows[:, bass.ds(2 * s.g, 2), :],
                             x_pairs[bass.ds(s.g, 1)].rearrange("g p k d -> p (g k) d")).then_inc(x_in[s.parity], 16)

            def load_residual(s):
                at_least(sp, post_done, s.tile(0) - 2)
                sp.dma_start(io[:, s.parity], x_pairs[bass.ds(s.g, 1)].rearrange("g p k d -> p (g k) d"))\
                  .then_inc(residual_in[s.parity], 16)

            def load_adj(s):
                if s.ahead(-1).bounded:
                    at_least(sp, masked_done, s.before_bounded())
                else:
                    sp.wait_ge(edge_done, s.n)
                sp.dma_start(adj_in[:, :, :, :], adj[:, bass.ds(2 * s.g, 2), :, :]).then_inc(adj_arrived, 16)

            def load_piece(phase, i):
                n = (phase - 1) * PIECES + i
                at_least(sp, piece_lo, n - 1)
                sp.dma_start(piece[:, n % 2], weights[phase, i]).then_inc(piece_in[n % 2], 16)

            def load_side_rows(phase):
                for side in (LEFT, RIGHT):
                    at_least(sp, side_biased[side], 2 * PAIRS * phase)
                    sp.dma_start(vector_rows[:, ROW_LEFT + side], vectors[phase, ROW_LEFT + side].partition_broadcast(P))\
                      .then_inc(side_rows_in, 16)

            def load_self_row(phase):
                at_least(sp, self_bias_scaled, 2 * PAIRS * phase)
                sp.dma_start(vector_rows[:, ROW_SELF], vectors[phase, ROW_SELF].partition_broadcast(P)).then_inc(self_row_in, 16)

            def load_norm_rows(phase):
                at_least(sp, post_done, 2 * PAIRS * phase)
                for v in (ROW_GAMMA, ROW_BETA):
                    sp.dma_start(vector_rows[:, v], vectors[phase, v].partition_broadcast(P)).then_inc(norm_rows_in, 16)

            def store(s):
                at_least(sp, post_done, s.tile(2))
                sp.dma_start(out_pairs[bass.ds(s.g, 1)].rearrange("g p k d -> p (g k) d"), io[:, s.parity])\
                  .then_inc(out_written[s.parity], 16)

            def body(s):
                prev, nxt, after = s.ahead(-1), s.ahead(1), s.ahead(2)
                if isinstance(s.n, int) and s.g == 0 and s.phase > 0:
                    load_side_rows(s.phase)
                    load_self_row(s.phase)
                if after.exists() and after.phase == 0:
                    load_x(after)
                if nxt.exists():
                    load_adj(nxt)
                for phase, i in pieces_of(s):
                    load_piece(phase, i)
                if nxt.exists() and nxt.phase == 1:
                    load_residual(nxt)
                if isinstance(s.n, int) and s.g == 0 and s.phase > 0:
                    load_norm_rows(s.phase)
                if prev.exists() and prev.phase == 2:
                    store(prev)

            def load_first(w):
                sp.dma_start(first_raw[:, w * CH:(w + 1) * CH], weights[0, w * CH:(w + 1) * CH].rearrange("c p e -> p c e"))\
                  .then_inc(first_in[w], 16)

            load_x(Step(0, 0, 0))
            sp.dma_start(self_rows[:, 0:P], identity).then_inc(identity_in, 16)
            load_first(RIGHT)
            load_x(Step(0, 0, 1))
            load_first(LEFT)
            load_adj(Step(0, 0, 0))
            sp.dma_start(tri[:, :, :], triangles).then_inc(triangles_in, 16)
            load_side_rows(0)
            load_first(SELF)
            load_self_row(0)
            load_norm_rows(0)
            walk(sp, body)
            final = Step(2, STEPS // 2 - 1, 1)
            for k in range(2):
                sp.wait_ge(post_done, final.tile(k) + 1)
                sp.dma_start(out_pairs[final.g, :, k], io[:, final.parity, k]).then_inc(out_written[final.parity], 16)
            sp.wait_ge(out_written[0], 16 * PAIRS // 2)
            sp.wait_ge(out_written[1], 16 * (PAIRS // 2 + 1))

        @block.tensor
        def _(pe):
            def transpose_nodes(s, k):
                pe.wait_ge(source_ready, s.tile(k) + 1)
                at_least(pe, node_lo, s.tile(k) - 1)
                for c in range(CH):
                    mm = nc.tensor.transpose(node_bank[k][:, c * P:(c + 1) * P], source[:, k, c * P:(c + 1) * P], ident)
                mm.then_inc(node_moved, 1)

            def scores(s):
                pe.wait_ge(node_hi, s.tile(2))
                pe.wait_ge(node_lo, s.tile(2))
                at_least(pe, score_summed, 2 * s.n)
                for k in range(2):
                    for c in range(CH):
                        t = node_t[:, s.parity, k, c].rearrange("p a r -> p (a r)")
                        mm = nc.tensor.matmul(score_bank[:, k * 256:(k + 1) * 256], t[:, 0:P], t,
                                              start=(k == 0 and c == 0), stop=(c == CH - 1), skip_group_check=True)
                mm.then_inc(scored, 1)

            def turn_cross(s):
                pe.wait_ge(cross_copied, s.n + 1)
                for k in range(2):
                    mm = nc.tensor.matmul(score_bank[:, k * 256:k * 256 + P], cross[:, k], ident_r[:, :],
                                          start=False, stop=True, skip_group_check=True)
                mm.then_inc(cross_turned, 1)

            def transpose_edges(s):
                pe.wait_ge(blocks_placed, 2 * s.n + 2)
                pe.wait_ge(attn_lo, s.n)
                for k in range(2):
                    for ul in range(2):
                        at = (2 * k + ul) * P
                        mm = nc.tensor.transpose(edge_bank[:, at:at + P], edge_block[:, k, ul], ident)
                mm.then_inc(edges_moved, 1)

            def project(s, k, w, bank, done):
                for c in range(CH):
                    for a, b in ((HI, HI), (HI, LO), (LO, HI)):
                        last = (c, a) == (CH - 1, LO)
                        mm = nc.tensor.matmul(bank[:, 0:D], node_t[:, s.parity, k, c, a], weight[:, s.phase % 2, w, c, b],
                                              start=(c == 0 and a == b), stop=last)
                mm.then_inc(done, 1)

            def weights_split(s, k, w):
                if isinstance(s.n, int) and s.g == 0 and k == 0:
                    if s.phase == 0:
                        pe.wait_ge(first_lo[w], CH)
                    else:
                        pe.wait_ge(piece_lo, (s.phase - 1) * PIECES + (w + 1) * CH)

            def project_side(s, k, side):
                pe.wait_ge(node_hi, s.tile(k) + 1)
                pe.wait_ge(node_lo, s.tile(k) + 1)
                at_least(pe, side_biased[side], s.tile(k))
                weights_split(s, k, side)
                project(s, k, side, side_bank[side], side_product[side])

            def project_self(s, k):
                at_least(pe, self_scaled, s.tile(k))
                weights_split(s, k, SELF)
                project(s, k, SELF, self_bank, self_product)

            def weigh(s, k):
                pe.wait_ge(attn_hi, s.n + 1)
                pe.wait_ge(attn_lo, s.n + 1)
                at_least(pe, context_done, s.tile(k))
                for side in (RIGHT, LEFT):
                    triangle = 1 - side if s.bounded else side
                    pe.wait_ge(side_hi[side], s.tile(k) + 1)
                    pe.wait_ge(side_lo[side], s.tile(k) + 1)
                    for a, b in ((HI, HI), (HI, LO), (LO, HI)):
                        mm = nc.tensor.matmul(context_bank[:, 0:D], attn_t[:, a, k, triangle], side_parts[:, side, b],
                                              start=(side == RIGHT and a == b), stop=(side == LEFT and a == LO))
                mm.then_inc(context_product, 1)

            def body(s):
                prev, nxt = s.ahead(-1), s.ahead(1)
                project_side(s, 0, RIGHT)
                project_side(s, 0, LEFT)
                if nxt.exists():
                    transpose_nodes(nxt, 0)
                if prev.exists():
                    weigh(prev, 1)
                if nxt.exists():
                    transpose_nodes(nxt, 1)
                project_self(s, 0)
                project_side(s, 1, RIGHT)
                if not s.bounded:
                    transpose_edges(s)
                if nxt.exists():
                    scores(nxt)
                project_side(s, 1, LEFT)
                if nxt.exists():
                    turn_cross(nxt)
                weigh(s, 0)
                project_self(s, 1)

            def keep_busy(products):
                for _ in range(products):
                    nc.tensor.matmul(edge_bank[:, :], edge_block[:, 0, 0],
                                     edge_block[:, :, :, :].rearrange("p k u r -> p (k u r)"), start=True, stop=True)

            pe.wait_ge(consts_set, 1)
            keep_busy(WARM_UP)
            pe.wait_ge(ident_rounded, 1)
            start = Step(0, 0, 0)
            transpose_nodes(start, 0)
            transpose_nodes(start, 1)
            keep_busy(1)
            scores(start)
            keep_busy(1)
            turn_cross(start)
            walk(pe, body)
            weigh(Step(2, STEPS // 2 - 1, 1), 1)

        @block.scalar
        def _(act):
            def fill_source(s, k):
                at_least(act, node_moved, s.tile(k) - 1)
                if s.phase == 1:
                    nc.scalar.activation(source[:, k:k + 1], rows[:, s.slot(k)], ACT.Copy).then_inc(source_ready, 1)
                else:
                    act.wait_ge(in_shift_done, s.normal + 1)
                    nc.scalar.activation(source[:, k:k + 1], rows[:, s.slot(k)], ACT.Identity, bias=in_shift[:, k:k + 1],
                                         scale=in_rstd[:, k:k + 1]).then_inc(source_ready, 1)

            def split_nodes(s, k):
                act.wait_ge(node_moved, s.tile(k) + 1)
                nc.scalar.activation(node_t[:, s.parity, k, :, HI], node_3[k], ACT.Relu).then_inc(node_hi, 1)

            def copy_cross(s):
                act.wait_ge(scored, s.n + 1)
                at_least(act, score_summed, 2 * s.n)
                nc.scalar.activation(cross[:, :, :], scores4[:, :, 1, :], ACT.Copy).then_inc(cross_copied, 1)

            def exponentials(s):
                if s.bounded:
                    act.wait_ge(score_summed, 2 * s.n + 2)
                else:
                    act.wait_ge(shift_done, s.n + 1 - PAIRS)
                for k in range(2):
                    nc.scalar.activation(score[:, k], score[:, k], ACT.Exp, scale=SCALE,
                                         accum_out=total[:, s.parity, k:k + 1]).then_inc(exp_done, 1)

            def place_blocks(s):
                act.wait_ge(edge3_done, s.n + 1)
                if s.ahead(-1).bounded:
                    at_least(act, attn_lo, s.n)
                else:
                    act.wait_ge(edges_moved, s.n - PAIRS)
                for h, half in enumerate(HALVES):
                    nc.scalar.activation(edge_block[half, :, :, h * NODES:(h + 1) * NODES], edge3[half, :, 0:2], ACT.Copy)\
                      .then_inc(blocks_placed, 1)

            def split_edges(s):
                if s.bounded:
                    act.wait_ge(blocks_placed, 2 * s.n + 2)
                    at_least(act, context_product, s.tile(0))
                    blocks = edge_block[:, :, :, :].rearrange("p k u r -> p (k u r)")
                else:
                    act.wait_ge(edges_moved, s.n + 1 - PAIRS)
                    blocks = edge_bank[:, :]
                nc.scalar.activation(attn_t[:, HI].rearrange("p k u r -> p (k u r)"), blocks, ACT.Copy).then_inc(attn_hi, 1)

            def split_side(s, k, side):
                act.wait_ge(side_biased[side], s.tile(k) + 1)
                at_least(act, context_product, s.tile(k))
                nc.scalar.activation(side_parts[:, side, HI], side_rows[:, side], ACT.Copy).then_inc(side_hi[side], 1)

            def scale_self(s, k):
                act.wait_ge(self_product, s.tile(k) + 1)
                act.wait_ge(diag_done, s.n + 1)
                at_least(act, self_biased, s.tile(k))
                nc.scalar.activation(self_rows[:, :], self_bank[:, 0:D], ACT.Identity,
                                     scale=diag[:, s.parity, k:k + 1]).then_inc(self_scaled, 1)

            def scale_self_bias(s, k):
                act.wait_ge(diag_done, s.n + 1)
                at_least(act, post_done, s.tile(k) - 1)
                if isinstance(s.n, int) and s.g == 0:
                    act.wait_ge(self_row_in, 16 * (s.phase + 1))
                nc.scalar.activation(context[:, k], vector_rows[:, ROW_SELF], ACT.Identity,
                                     scale=diag[:, s.parity, k:k + 1]).then_inc(self_bias_scaled, 1)

            def split_piece(phase, i):
                n = (phase - 1) * PIECES + i
                act.wait_ge(piece_in[n % 2], 16 * (n // 2 + 1))
                nc.scalar.activation(piece_part(phase, i, HI), piece[:, n % 2], ACT.Copy).then_inc(piece_hi, 1)

            def split_first(w):
                act.wait_ge(first_in[w], 16)
                for i in range(w * CH, (w + 1) * CH):
                    nc.scalar.activation(piece_part(0, i, HI), first_raw[:, i], ACT.Copy).then_inc(first_hi[w], 1)

            def body(s):
                nxt, after = s.ahead(1), s.ahead(2)
                pieces = pieces_of(s)
                if nxt.exists():
                    split_nodes(nxt, 0)
                split_side(s, 0, RIGHT)
                if nxt.exists():
                    split_nodes(nxt, 1)
                place_blocks(s)
                split_side(s, 0, LEFT)
                split_edges(s)
                if nxt.exists():
                    copy_cross(nxt)
                scale_self(s, 0)
                if len(pieces) > 0:
                    split_piece(*pieces[0])
                scale_self_bias(s, 0)
                split_side(s, 1, LEFT)
                split_side(s, 1, RIGHT)
                if len(pieces) > 1:
                    split_piece(*pieces[1])
                if nxt.exists():
                    exponentials(nxt)
                if after.exists():
                    fill_source(after, 0)
                scale_self(s, 1)
                scale_self_bias(s, 1)
                if after.exists():
                    fill_source(after, 1)

            act.wait_ge(identity_in, 16)
            nc.scalar.activation(ident_r[:, :], self_rows[:, 0:P], ACT.Copy).then_inc(ident_rounded, 1)
            start = Step(0, 0, 0)
            fill_source(start, 0)
            fill_source(start, 1)
            act.wait_ge(consts_set, 1)
            split_nodes(start, 0)
            split_nodes(start, 1)
            split_first(RIGHT)
            copy_cross(start)
            split_first(LEFT)
            fill_source(start.ahead(1), 0)
            exponentials(start)
            fill_source(start.ahead(1), 1)
            split_first(SELF)
            walk(act, body)

        @block.vector
        def _(dve):
            def input_stats(s, k):
                if s.phase == 0:
                    dve.wait_ge(x_in[s.parity], 16 * (s.half + 1))
                at_least(dve, in_rstd_done, s.normal)
                nc.vector.bn_stats(in_stats[:, k], rows[:, s.slot(k)]).then_inc(in_stats_raw, 1)

            def gather_input(s, k):
                dve.wait_ge(in_stats_raw, 2 * s.normal + k + 1)
                nc.vector.memset(gate[:, k:k + 1], 0.0)
                nc.vector.bn_aggr(in_moments[:, k], in_stats[:, k]).then_inc(in_stats_done, 1)

            def input_shift(s):
                dve.wait_ge(in_rstd_done, s.normal + 1)
                at_least(dve, source_ready, s.tile(0))
                nc.vector.scalar_tensor_tensor(in_shift[:, :], in_moments[:, :, 0], -1.0, in_rstd[:, :],
                                               ALU.mult, ALU.mult).then_inc(in_shift_done, 1)

            def split_nodes(s, k):
                dve.wait_ge(node_hi, s.tile(k) + 1)
                nc.vector.scalar_tensor_tensor(node_t[:, s.parity, k, :, LO], node_3[k], 0.0,
                                               node_t[:, s.parity, k, :, HI].bitcast(F32),
                                               ALU.max, ALU.subtract).then_inc(node_lo, 1)

            def sum_scores(s):
                dve.wait_ge(cross_turned, s.n + 1)
                for h, half in enumerate(HALVES):
                    nc.vector.tensor_tensor(score[half], scores4[half, :, 0, h * NODES:(h + 1) * NODES],
                                            cross[half, :, h * NODES:(h + 1) * NODES].bitcast(F32),
                                            ALU.add).then_inc(score_summed, 1)

            def row_maximum(s):
                dve.wait_ge(score_summed, 2 * s.n + 2)
                nc.vector.tensor_reduce(row_max[:, :], score[:, :, :], op=ALU.max, axis=AX.X).then_inc(max_done, 1)

            def shift_scores(s):
                dve.wait_ge(max_done, s.n + 1 - PAIRS)
                nc.vector.tensor_tensor(score[:, :, :], score[:, :, :],
                                        row_max[:, :].unsqueeze(2).to_broadcast([P, 2, NODES]),
                                        ALU.subtract).then_inc(shift_done, 1)

            def mask_edges(s):
                dve.wait_ge(exp_done, 2 * s.n + 2)
                dve.wait_ge(adj_arrived, 16 * (s.n + 1))
                at_least(dve, edge3_done, s.n)
                nc.vector.tensor_tensor(edge[:, :, :], score[:, :, :], adj_in[:, :, int(s.bounded)], ALU.mult).then_inc(edge_done, 1)

            def mask_rows(s):
                nc.vector.tensor_tensor(score[:, :, :], score[:, :, :], adj_in[:, :, 0], ALU.mult).then_inc(masked_done, 1)

            def sum_kept(s):
                if s.bounded:
                    dve.wait_ge(masked_done, s.before_bounded() + 1)
                else:
                    dve.wait_ge(edge_done, s.n + 1)
                masked = score[:, :, :] if s.bounded else edge[:, :, :]
                nc.vector.tensor_reduce(kept[:, :], masked, op=ALU.add, axis=AX.X).then_inc(kept_done, 1)

            def denominator(s):
                dve.wait_ge(kept_done, s.n + 1)
                nc.vector.scalar_tensor_tensor(den[:, :], total[:, s.parity], GUARD, kept[:, :],
                                               ALU.mult, ALU.add).then_inc(den_done, 1)

            def diagonal(s):
                dve.wait_ge(edge3_done, s.n + 1)
                nc.vector.tensor_reduce(diag[:, s.parity], edge3[:, :, 2], op=ALU.add, axis=AX.X).then_inc(diag_done, 1)

            def squared_denominator(s):
                dve.wait_ge(den_done, s.n + 1)
                nc.vector.tensor_tensor(den_sq[:, s.parity], den[:, :], den[:, :], ALU.mult).then_inc(den_sq_done, 1)

            def split_first(w):
                for i in range(CH):
                    dve.wait_ge(first_hi[w], i + 1)
                    nc.vector.tensor_tensor(piece_part(0, w * CH + i, LO), first_raw[:, w * CH + i],
                                            piece_part(0, w * CH + i, HI).bitcast(F32), ALU.subtract).then_inc(first_lo[w], 1)

            def split_edges(s):
                dve.wait_ge(attn_hi, s.n + 1)
                blocks = edge_block[:, :, :, :].rearrange("p k u r -> p (k u r)") if s.bounded else edge_bank[:, :]
                nc.vector.tensor_tensor(attn_t[:, LO].rearrange("p k u r -> p (k u r)"), blocks,
                                        attn_t[:, HI].rearrange("p k u r -> p (k u r)").bitcast(F32),
                                        ALU.subtract).then_inc(attn_lo, 1)

            def add_bias(s, k, side):
                dve.wait_ge(side_product[side], s.tile(k) + 1)
                at_least(dve, side_lo[side], s.tile(k))
                if isinstance(s.n, int) and s.g == 0:
                    dve.wait_ge(side_rows_in, 32 * (s.phase + 1))
                nc.vector.tensor_tensor(side_rows[:, side], side_bank[side][:, 0:D], vector_rows[:, ROW_LEFT + side],
                                        ALU.add).then_inc(side_biased[side], 1)

            def sum_context(s, k):
                dve.wait_ge(context_product, s.tile(k) + 1)
                dve.wait_ge(self_biased, s.tile(k) + 1)
                nc.vector.tensor_tensor(context[:, k], context_bank[:, 0:D], context[:, k], ALU.add).then_inc(context_done, 1)

            def context_stats(s, k):
                dve.wait_ge(context_done, s.tile(k) + 1)
                nc.vector.bn_stats(stats[:, k], context[:, k]).then_inc(stats_done, 1)

            def gather_moments(s, k):
                dve.wait_ge(stats_done, s.tile(k) + 1)
                nc.vector.memset(gate[:, 2 + k:3 + k], 0.0)
                nc.vector.bn_aggr(moments[:, k], stats[:, k]).then_inc(moments_done, 1)

            def spreads(s):
                dve.wait_ge(moments_done, s.tile(2))
                dve.wait_ge(den_sq_done, s.n + 1)
                nc.vector.scalar_tensor_tensor(spread[:, :], den_sq[:, s.parity], GNN_EPS, moments[:, :, 1],
                                               ALU.mult, ALU.add).then_inc(spread_done, 1)

            def centre(s, k):
                if isinstance(s.n, int) and s.g == 0:
                    dve.wait_ge(norm_rows_in, 32 * (s.phase + 1))
                dve.wait_ge(moments_done, s.tile(k) + 1)
                nc.vector.scalar_tensor_tensor(context[:, k], context[:, k], moments[:, k, 0:1], vector_rows[:, ROW_GAMMA],
                                               ALU.subtract, ALU.mult).then_inc(centred, 1)

            def norm(s, k):
                dve.wait_ge(rstd_done, s.n + 1)
                dve.wait_ge(centred, s.tile(k) + 1)
                to, done = (rows[:, s.slot(k)], post_done) if s.phase == 0 else (context[:, k:k + 1], normed)
                nc.vector.scalar_tensor_tensor(to, context[:, k:k + 1], rstd[:, k:k + 1], vector_rows[:, ROW_BETA:ROW_BETA + 1],
                                               ALU.mult, ALU.add).then_inc(done, 1)

            def residual(s, k):
                dve.wait_ge(normed, s.tile(k) + 1 - 2 * PAIRS)
                if s.phase == 1:
                    dve.wait_ge(residual_in[s.parity], 16 * (s.half + 1 - PAIRS // 2))
                    other, to = io[:, s.parity, k:k + 1], rows[:, s.slot(k)]
                else:
                    at_least(dve, out_written[s.parity], 16 * (s.half - PAIRS))
                    other, to = rows[:, s.slot(k)], io[:, s.parity, k:k + 1]
                nc.vector.scalar_tensor_tensor(to, context[:, k:k + 1], 0.0, other, ALU.max, ALU.add).then_inc(post_done, 1)

            def body(s):
                prev, nxt, after = s.ahead(-1), s.ahead(1), s.ahead(2)
                if after.exists() and after.bounded:
                    input_stats(after, 0)
                if prev.exists():
                    centre(prev, 0)
                add_bias(s, 0, LEFT)
                add_bias(s, 0, RIGHT)
                if prev.exists():
                    sum_context(prev, 1)
                denominator(s)
                if after.exists() and after.bounded:
                    gather_input(after, 0)
                if prev.exists():
                    context_stats(prev, 1)
                if nxt.exists():
                    split_nodes(nxt, 0)
                if prev.exists():
                    gather_moments(prev, 1)
                if nxt.exists():
                    split_nodes(nxt, 1)
                if prev.exists():
                    spreads(prev)
                if after.exists() and after.bounded:
                    input_stats(after, 1)
                if prev.exists():
                    centre(prev, 1)
                diagonal(s)
                squared_denominator(s)
                if prev.exists():
                    norm(prev, 0)
                split_edges(s)
                if after.exists() and after.bounded:
                    gather_input(after, 1)
                if prev.exists() and prev.phase > 0:
                    residual(prev, 0)
                add_bias(s, 1, LEFT)
                add_bias(s, 1, RIGHT)
                if nxt.exists():
                    sum_scores(nxt)
                if nxt.exists() and not nxt.bounded:
                    row_maximum(nxt)
                    shift_scores(nxt)
                if prev.exists():
                    norm(prev, 1)
                if after.exists() and after.bounded:
                    input_shift(after)
                if prev.exists() and prev.phase > 0:
                    residual(prev, 1)
                sum_context(s, 0)
                if nxt.exists():
                    mask_edges(nxt)
                if nxt.exists() and nxt.bounded:
                    mask_rows(nxt)
                context_stats(s, 0)
                if nxt.exists():
                    sum_kept(nxt)
                gather_moments(s, 0)

            start = Step(0, 0, 0)
            nc.vector.memset(edge_block[:, :, :, :], 0.0)
            nc.vector.memset(minus_half[:, :], -0.5)
            nc.vector.memset(ln_eps[:, :], LN_EPS).then_inc(consts_set, 1)
            for k in range(2):
                input_stats(start, k)
                gather_input(start, k)
            input_shift(start)
            for k in range(2):
                input_stats(start.ahead(1), k)
                gather_input(start.ahead(1), k)
            split_nodes(start, 0)
            split_nodes(start, 1)
            split_first(RIGHT)
            input_shift(start.ahead(1))
            sum_scores(start)
            split_first(LEFT)
            mask_edges(start)
            mask_rows(start)
            sum_kept(start)
            split_first(SELF)
            walk(dve, body)
            final = Step(2, STEPS // 2 - 1, 1)
            sum_context(final, 1)
            context_stats(final, 1)
            centre(final, 0)
            gather_moments(final, 1)
            spreads(final)
            centre(final, 1)
            for k in range(2):
                norm(final, k)
                residual(final, k)

        @block.gpsimd
        def _(pool):
            def input_rstd(s):
                pool.wait_ge(in_stats_done, 2 * s.normal + 2)
                at_least(pool, source_ready, s.tile(0))
                nc.gpsimd.tensor_tensor(in_spread[:, :], in_moments[:, :, 1], ln_eps[:, :], ALU.add).then_inc(in_spread_done, 1)
                pool.wait_ge(in_spread_done, s.normal + 1)
                nc.gpsimd.tensor_tensor(in_rstd[:, :], in_spread[:, :], minus_half[:, :], ALU.pow).then_inc(in_rstd_done, 1)

            def output_rstd(s):
                pool.wait_ge(spread_done, s.n + 1)
                nc.gpsimd.tensor_tensor(rstd[:, :], spread[:, :], minus_half[:, :], ALU.pow).then_inc(rstd_done, 1)

            def split_side(s, k, side):
                pool.wait_ge(side_hi[side], s.tile(k) + 1)
                nc.gpsimd.tensor_tensor(side_parts[:, side, LO], side_rows[:, side], side_parts[:, side, HI].bitcast(F32),
                                        ALU.subtract).then_inc(side_lo[side], 1)

            def bias_self(s, k):
                pool.wait_ge(self_scaled, s.tile(k) + 1)
                pool.wait_ge(self_bias_scaled, s.tile(k) + 1)
                nc.gpsimd.tensor_tensor(context[:, k], self_rows[:, :], context[:, k], ALU.add).then_inc(self_biased, 1)

            def triangles_of(s):
                pool.wait_ge(edge_done, s.n + 1)
                at_least(pool, blocks_placed, 2 * s.n)
                at_least(pool, diag_done, s.n)
                nc.gpsimd.tensor_tensor(edge3[:, :, :, :], edge[:, :, :].unsqueeze(2).to_broadcast([P, 2, 3, NODES]),
                                        tri[:, :, :].unsqueeze(1).to_broadcast([P, 2, 3, NODES]), ALU.mult).then_inc(edge3_done, 1)

            def split_piece(phase, i):
                n = (phase - 1) * PIECES + i
                pool.wait_ge(piece_hi, n + 1)
                nc.gpsimd.tensor_tensor(piece_part(phase, i, LO), piece[:, n % 2], piece_part(phase, i, HI).bitcast(F32),
                                        ALU.subtract).then_inc(piece_lo, 1)

            def body(s):
                prev, nxt, after = s.ahead(-1), s.ahead(1), s.ahead(2)
                pieces = pieces_of(s)
                split_side(s, 0, RIGHT)
                if prev.exists():
                    output_rstd(prev)
                split_side(s, 0, LEFT)
                if after.exists() and after.bounded:
                    input_rstd(after)
                bias_self(s, 0)
                if len(pieces) > 0:
                    split_piece(*pieces[0])
                split_side(s, 1, RIGHT)
                split_side(s, 1, LEFT)
                bias_self(s, 1)
                if len(pieces) > 1:
                    split_piece(*pieces[1])
                if nxt.exists():
                    triangles_of(nxt)

            pool.wait_ge(consts_set, 1)
            start = Step(0, 0, 0)
            input_rstd(start)
            input_rstd(start.ahead(1))
            pool.wait_ge(triangles_in, 16)
            triangles_of(start)
            walk(pool, body)
            output_rstd(Step(2, STEPS // 2 - 1, 1))


def kernel(**inputs):
    import numpy as np
    import concourse.bacc as bacc
    from concourse.bass_utils import run_bass_kernel_spmd

    given = {name: np.asarray(value) for name, value in inputs.items()}

    def layer(kind, name):
        return [given["L0_gnn_" + kind[0]][0], given["L0_gnn_" + kind[0]][1], given["L1_gnn_" + kind[1]]][name]

    matrices = [[layer(kind, n) for kind in (("Wl", "W_left"), ("Wr", "W_right"), ("Ws", "W_self"))] for n in range(PHASES)]
    rows = [[layer(kind, n) for kind in (("ln_w", "gamma"), ("ln_b", "beta"), ("bl", "b_left"), ("br", "b_right"), ("bs", "b_self"))]
            for n in range(PHASES)]
    below = np.tril(np.ones((NODES, NODES), np.float32), -1)
    triangles = np.stack([below.T, below, np.eye(NODES, dtype=np.float32)], axis=1)
    arrays = {
        "x": np.ascontiguousarray(given["x"].reshape(TILES * P, D)),
        "adj": np.ascontiguousarray(np.stack([given["adj"], given["adj"].transpose(0, 2, 1)], axis=2)
                                    .reshape(TILES, P, 2, NODES).transpose(1, 0, 2, 3)),
        "weights": np.ascontiguousarray(np.stack([np.stack([m.T.reshape(CH, P, D) for m in ms]) for ms in matrices])
                                        .reshape(PHASES, 3 * CH, P, D)),
        "vectors": np.ascontiguousarray(np.stack([np.stack(r) for r in rows])),
        "identity": np.eye(P, dtype=np.float32),
        "triangles": np.concatenate([triangles, triangles]),
    }
    nc = bacc.Bacc("TRN2", target_bir_lowering=False, num_devices=1)
    aps = [nc.dram_tensor(name, a.shape, mybir.dt.from_np(a.dtype), kind="ExternalInput").ap() for name, a in arrays.items()]
    out = nc.dram_tensor("out", (TILES * P, D), F32, kind="ExternalOutput").ap()
    adj_gnn_program(nc, *aps, out)
    result = run_bass_kernel_spmd(nc, [arrays], core_ids=[0])
    return result.results[0]["out"].reshape(TILES * P // NODES, NODES, D)
```
